# Optimizing a Trainium2 kernel written in Bass

```python
import numpy as np
import jax
import jax.numpy as jnp

def _softmax(x, axis=-1):
    return jax.nn.softmax(x, axis=axis)

def _gelu(x):
    return jax.nn.gelu(x, approximate=True)

def _silu(x):
    return jax.nn.silu(x)

def _sigmoid(x):
    return jax.nn.sigmoid(x)

def _layernorm(x, axis=-1, eps=1e-05):
    m = jnp.mean(x, axis=axis, keepdims=True)
    v = jnp.var(x, axis=axis, keepdims=True)
    return (x - m) / jnp.sqrt(v + eps)

def _scatter_add(tgt, idx, src, axis=0):
    return tgt.at[idx].add(src)

def _segment_sum(src, seg, n):
    return jax.ops.segment_sum(src, seg, n)
kernel_name = 'mk_adj_preln_d4_adj_r2_c7b0a1'

def setup_inputs(seed: int=0):
    np.random.seed(seed)
    _w = jnp.asarray

    def _rec_inputs():
        import jax
        import jax.numpy as jnp
        _gk = jax.random.key(seed)
        x = -0.0005207 + 1.001 * jax.random.normal(jax.random.fold_in(_gk, 1), (8, 1024, 128), jnp.float32)
        _a = jax.random.bernoulli(jax.random.fold_in(_gk, 2), 0.0078125, (8, 1024, 1024))
        adj = _a.astype(jnp.int32)
        return (x, adj)
    x, adj = _rec_inputs()

    def _L0_gnn_setup():
        import jax, jax.numpy as jnp
        import numpy as np
        DIM = 128
        HEADS = 4
        B, N = (2, 2048)
        NEG = -1000000000.0
        EPS = 1e-05
        key = jax.random.key(seed)
        ks = jax.random.split(key, 12)
        s = 0.02
        inp = {'x': jax.random.normal(ks[0], (B, N, DIM), dtype=jnp.float32), 'adj': jax.random.randint(ks[1], (B, N, N), 0, 2, dtype=jnp.int32), 'Wq': jax.random.normal(ks[2], (DIM, DIM), dtype=jnp.float32) * s, 'bq': jnp.zeros((DIM,), jnp.float32), 'Wk': jax.random.normal(ks[3], (DIM, DIM), dtype=jnp.float32) * s, 'bk': jnp.zeros((DIM,), jnp.float32), 'Wv': jax.random.normal(ks[4], (DIM, DIM), dtype=jnp.float32) * s, 'bv': jnp.zeros((DIM,), jnp.float32), 'Wo': jax.random.normal(ks[5], (DIM, DIM), dtype=jnp.float32) * s, 'bo': jnp.zeros((DIM,), jnp.float32), 'gamma': jnp.ones((DIM,), jnp.float32), 'beta': jnp.zeros((DIM,), jnp.float32)}
        return inp
    _L0_gnn_all = _L0_gnn_setup()
    _L0_gnn_in = {k: v for k, v in _L0_gnn_all.items() if k in ('Wq', 'bq', 'Wk', 'bk', 'Wv', 'bv', 'Wo', 'bo', 'gamma', 'beta')}
    del _L0_gnn_all

    def _L1_gnn_setup():
        import jax, jax.numpy as jnp
        import numpy as np
        OUT = 128
        NUM_LAYERS = 3

        def _gru_cell(inp, h, w_ih, w_hh, b_ih, b_hh):
            gi = inp @ w_ih.T + b_ih
            gh = h @ w_hh.T + b_hh
            i_r, i_z, i_n = jnp.split(gi, 3, axis=-1)
            h_r, h_z, h_n = jnp.split(gh, 3, axis=-1)
            r = jax.nn.sigmoid(i_r + h_r)
            z = jax.nn.sigmoid(i_z + h_z)
            n = jnp.tanh(i_n + r * h_n)
            return (1.0 - z) * n + z * h
        key = jax.random.key(seed)
        ks = jax.random.split(key, 8)
        B, N, D = (32, 256, 128)
        x = jax.random.normal(ks[0], (B, N, D), dtype=jnp.float32)
        adj = jax.random.randint(ks[1], (B, N, N), 0, 2, dtype=jnp.int32)
        s = 1.0 / np.sqrt(OUT)
        weight = jax.random.uniform(ks[2], (NUM_LAYERS, OUT, OUT), jnp.float32, -s, s)
        w_ih = jax.random.uniform(ks[3], (3 * OUT, OUT), jnp.float32, -s, s)
        w_hh = jax.random.uniform(ks[4], (3 * OUT, OUT), jnp.float32, -s, s)
        b_ih = jax.random.uniform(ks[5], (3 * OUT,), jnp.float32, -s, s)
        b_hh = jax.random.uniform(ks[6], (3 * OUT,), jnp.float32, -s, s)
        return {'x': x, 'adj': adj, 'weight': weight, 'w_ih': w_ih, 'w_hh': w_hh, 'b_ih': b_ih, 'b_hh': b_hh}
    _L1_gnn_all = _L1_gnn_setup()
    _L1_gnn_in = {k: v for k, v in _L1_gnn_all.items() if k in ('weight', 'w_ih', 'w_hh', 'b_ih', 'b_hh')}
    del _L1_gnn_all

    def _L2_gnn_setup():
        import jax, jax.numpy as jnp
        import numpy as np
        B, N, C, OUT, S = (4, 1024, 128, 128, 25)
        DENSITY = 0.008
        key = jax.random.key(seed)
        kA, kX, kW = jax.random.split(key, 3)
        A = jax.random.bernoulli(kA, DENSITY, (B, N, N)).astype(jnp.int32)
        X = jax.random.normal(kX, (B, N, C), dtype=jnp.float32)
        W = jax.random.normal(kW, (2 * C, OUT), dtype=jnp.float32) * np.float32(1.0 / np.sqrt(2 * C))
        b = jnp.zeros((OUT,), dtype=jnp.float32)
        return {'A': A, 'X': X, 'W': W, 'b': b}
    _L2_gnn_all = _L2_gnn_setup()
    _L2_gnn_in = {k: v for k, v in _L2_gnn_all.items() if k in ('W', 'b')}
    del _L2_gnn_all

    def _L3_gnn_setup():
        import jax, jax.numpy as jnp
        import numpy as np
        BS, N, D, R = (16, 256, 128, 2)
        key = jax.random.key(seed)
        ks = jax.random.split(key, 9)
        s = 1.0 / np.sqrt(D)
        return {'encoded_spans': jax.random.normal(ks[0], (BS, N, D), dtype=jnp.float32), 'w_rel1': jax.random.normal(ks[1], (R, D, D), dtype=jnp.float32) * s, 'w_root1': jax.random.normal(ks[2], (D, D), dtype=jnp.float32) * s, 'b1': jnp.zeros((D,), dtype=jnp.float32), 'w_rel2': jax.random.normal(ks[3], (R, D, D), dtype=jnp.float32) * s, 'w_root2': jax.random.normal(ks[4], (D, D), dtype=jnp.float32) * s, 'b2': jnp.zeros((D,), dtype=jnp.float32), 'aug_adj': jax.random.randint(ks[5], (BS, N, N), 0, 16, dtype=jnp.int64), 'punct_graph': jax.random.randint(ks[6], (BS, N, N), 0, 16, dtype=jnp.int64)}
    _L3_gnn_all = _L3_gnn_setup()
    _L3_gnn_in = {k: v for k, v in _L3_gnn_all.items() if k in ('w_rel1', 'w_root1', 'b1', 'w_rel2', 'w_root2', 'b2')}
    del _L3_gnn_all
    return {'x': x, 'adj': adj, 'L0_gnn_Wq': _L0_gnn_in['Wq'], 'L0_gnn_bq': _L0_gnn_in['bq'], 'L0_gnn_Wk': _L0_gnn_in['Wk'], 'L0_gnn_bk': _L0_gnn_in['bk'], 'L0_gnn_Wv': _L0_gnn_in['Wv'], 'L0_gnn_bv': _L0_gnn_in['bv'], 'L0_gnn_Wo': _L0_gnn_in['Wo'], 'L0_gnn_bo': _L0_gnn_in['bo'], 'L0_gnn_gamma': _L0_gnn_in['gamma'], 'L0_gnn_beta': _L0_gnn_in['beta'], 'L1_gnn_weight': _L1_gnn_in['weight'], 'L1_gnn_w_ih': _L1_gnn_in['w_ih'], 'L1_gnn_w_hh': _L1_gnn_in['w_hh'], 'L1_gnn_b_ih': _L1_gnn_in['b_ih'], 'L1_gnn_b_hh': _L1_gnn_in['b_hh'], 'L2_gnn_W': _L2_gnn_in['W'], 'L2_gnn_b': _L2_gnn_in['b'], 'L3_gnn_w_rel1': _L3_gnn_in['w_rel1'], 'L3_gnn_w_root1': _L3_gnn_in['w_root1'], 'L3_gnn_b1': _L3_gnn_in['b1'], 'L3_gnn_w_rel2': _L3_gnn_in['w_rel2'], 'L3_gnn_w_root2': _L3_gnn_in['w_root2'], 'L3_gnn_b2': _L3_gnn_in['b2']}

def reference(x, adj, L0_gnn_Wq, L0_gnn_bq, L0_gnn_Wk, L0_gnn_bk, L0_gnn_Wv, L0_gnn_bv, L0_gnn_Wo, L0_gnn_bo, L0_gnn_gamma, L0_gnn_beta, L1_gnn_weight, L1_gnn_w_ih, L1_gnn_w_hh, L1_gnn_b_ih, L1_gnn_b_hh, L2_gnn_W, L2_gnn_b, L3_gnn_w_rel1, L3_gnn_w_root1, L3_gnn_b1, L3_gnn_w_rel2, L3_gnn_w_root2, L3_gnn_b2):
    import jax
    import jax.numpy as jnp

    def _L0_gnn_ref(x, adj, Wq, bq, Wk, bk, Wv, bv, Wo, bo, gamma, beta):
        import jax, jax.numpy as jnp
        import numpy as np
        DIM = 128
        HEADS = 4
        B, N = (2, 2048)
        NEG = -1000000000.0
        EPS = 1e-05
        Bx, Nx, C = x.shape
        H = HEADS
        D = C // H
        scale = D ** (-0.5)

        def proj(W, b):
            return (x @ W.T + b).reshape(Bx, Nx, H, D).transpose(0, 2, 1, 3)
        q = proj(Wq, bq)
        k = proj(Wk, bk)
        v = proj(Wv, bv)
        attn = jnp.einsum('bhnd,bhmd->bhnm', q, k) * scale
        attn = jnp.where(adj[:, None, :, :] == 0, NEG, attn)
        attn = jax.nn.softmax(attn, axis=-1)
        out = jnp.einsum('bhnm,bhmd->bhnd', attn, v)
        out = out.transpose(0, 2, 1, 3).reshape(Bx, Nx, C)
        out = out @ Wo.T + bo
        mu = jnp.mean(out, axis=-1, keepdims=True)
        var = jnp.var(out, axis=-1, keepdims=True)
        return (out - mu) * jax.lax.rsqrt(var + EPS) * gamma + beta

    def _L1_gnn_ref(x, adj, weight, w_ih, w_hh, b_ih, b_hh):
        import jax, jax.numpy as jnp
        import numpy as np
        OUT = 128
        NUM_LAYERS = 3

        def _gru_cell(inp, h, w_ih, w_hh, b_ih, b_hh):
            gi = inp @ w_ih.T + b_ih
            gh = h @ w_hh.T + b_hh
            i_r, i_z, i_n = jnp.split(gi, 3, axis=-1)
            h_r, h_z, h_n = jnp.split(gh, 3, axis=-1)
            r = jax.nn.sigmoid(i_r + h_r)
            z = jax.nn.sigmoid(i_z + h_z)
            n = jnp.tanh(i_n + r * h_n)
            return (1.0 - z) * n + z * h
        A = (adj != 0).astype(x.dtype)
        h = x
        L = weight.shape[0]
        for i in range(L):
            m = jnp.einsum('bnd,de->bne', h, weight[i])
            aggr = jnp.einsum('bst,bsd->btd', A, m)
            h = _gru_cell(aggr, h, w_ih, w_hh, b_ih, b_hh)
        return h

    def _L2_gnn_ref(A, X, W, b):
        import jax, jax.numpy as jnp
        import numpy as np
        B, N, C, OUT, S = (4, 1024, 128, 128, 25)
        DENSITY = 0.008
        mask = A != 0
        neg_inf = jnp.float32(-jnp.inf)
        pri = -jnp.arange(N, dtype=jnp.float32)
        scores = jnp.where(mask, pri, neg_inf)
        vals, idx = jax.lax.top_k(scores, S)
        valid = vals > neg_inf
        feats = jax.vmap(lambda x, i: x[i])(X, idx)
        feats = jnp.where(valid[..., None], feats, neg_inf)
        agg = feats.max(axis=2)
        degree = mask.sum(axis=-1)
        agg = jnp.where((degree <= S)[..., None], jnp.maximum(agg, 0.0), agg)
        h = jnp.concatenate([X, agg], axis=-1)
        out = jax.nn.relu(jnp.einsum('bnf,fo->bno', h, W) + b)
        return out

    def _L3_gnn_ref(encoded_spans, w_rel1, w_root1, b1, w_rel2, w_root2, b2, aug_adj, punct_graph):
        import jax, jax.numpy as jnp
        import numpy as np
        BS, N, D, R = (16, 256, 128, 2)
        mask_punct = (punct_graph == 1) & (aug_adj != 1)
        mask_aug = aug_adj == 1
        masks = jnp.stack([mask_punct, mask_aug]).astype(encoded_spans.dtype)
        deg = jnp.maximum(masks.sum(axis=2), 1.0)[..., None]

        def conv(x, w_rel, w_root, b):
            out = jnp.einsum('bnd,de->bne', x, w_root) + b
            for r in range(R):
                agg = jnp.einsum('bij,bid->bjd', masks[r], x) / deg[r]
                out = out + jnp.einsum('bjd,de->bje', agg, w_rel[r])
            return out
        h = jax.nn.elu(conv(encoded_spans, w_rel1, w_root1, b1))
        h = jax.nn.elu(conv(h, w_rel2, w_root2, b2))
        return h
    h = jnp.maximum(_layernorm(x, axis=-1), 0.0)
    x = x + _L0_gnn_ref(h, adj, L0_gnn_Wq, L0_gnn_bq, L0_gnn_Wk, L0_gnn_bk, L0_gnn_Wv, L0_gnn_bv, L0_gnn_Wo, L0_gnn_bo, L0_gnn_gamma, L0_gnn_beta)
    h = jnp.maximum(_layernorm(x, axis=-1), 0.0)
    x = x + _L1_gnn_ref(h, adj, L1_gnn_weight, L1_gnn_w_ih, L1_gnn_w_hh, L1_gnn_b_ih, L1_gnn_b_hh)
    h = jnp.maximum(_layernorm(x, axis=-1), 0.0)
    x = x + _L2_gnn_ref(adj, h, L2_gnn_W, L2_gnn_b)
    h = jnp.maximum(_layernorm(x, axis=-1), 0.0)
    x = x + _L3_gnn_ref(h, L3_gnn_w_rel1, L3_gnn_w_root1, L3_gnn_b1, L3_gnn_w_rel2, L3_gnn_w_root2, L3_gnn_b2, adj, adj)
    return x

_drawn_inputs = setup_inputs


def setup_inputs(seed=0):
    import zlib

    import numpy as np

    out = dict(_drawn_inputs(seed))
    spreads = {'L0_gnn_bq': (0.0, 0.8),
     'L0_gnn_bk': (0.0, 0.8),
     'L0_gnn_bv': (0.0, 0.1),
     'L0_gnn_bo': (0.0, 0.1),
     'L0_gnn_gamma': (1.0, 0.2),
     'L0_gnn_beta': (0.0, 0.1),
     'L2_gnn_b': (0.0, 0.1),
     'L3_gnn_b1': (0.0, 0.1),
     'L3_gnn_b2': (0.0, 0.1)}
    factors = {'L0_gnn_Wq': 8.0, 'L0_gnn_Wk': 8.0, 'L1_gnn_b_hh': 3.587}
    for name, (base, spread) in spreads.items():
        noise = np.random.default_rng([zlib.crc32(name.encode()), seed]).standard_normal(out[name].shape)
        drawn = base * np.exp(spread * noise) if base else spread * noise
        out[name] = jnp.asarray(drawn.astype(out[name].dtype))
    for name, factor in factors.items():
        out[name] = (out[name] * factor).astype(out[name].dtype)
    return out
```

```python
import concourse.bass as bass
from concourse import mybir
from contextlib import ExitStack

P = 128
BATCH, NODES, DIM = 8, 1024, 128
TILES = NODES // P
HEADS = 4
HEAD = DIM // HEADS
HALF = 512
HALVES = NODES // HALF
PER_HALF = HALF // P
LAYERS = 3
CONVS = 2
GATES = 3
STEPS = TILES * HEADS
RING = 5
SLOTS = 25
BIG = 2.0 ** 100
EPS = 1e-5
F8_ONE = 0x38
NB = 3


ATTENTION = (
    [(("a_stats", 0), 3), (("a_norm",), 5), (("a_q",), 3), (("a_k",), 3), (("a_v",), 2)]
    + [(("a_step", s), 4.2) for s in range(STEPS + 2)]
    + [(("a_rinv",), 2), (("a_y",), 3), (("a_stats", 1), 4), (("a_ynorm",), 4), (("a_gain",), 5)])
OTHERS = (
    [(("b_stats", 1), 3), (("b_masks",), 3), (("b_norm", 1), 5)]
    + [w for layer in range(LAYERS) for w in (
        [(("b_gather", layer, j), 3.5) for j in range(HALVES)]
        + [(("b_gates", layer, j), 6) for j in range(HALVES)] + [(("b_natural", layer), 3)])]
    + [(("b_stats", 2), 3), (("b_limit",), 1), (("b_edgeT",), 4), (("b_norm", 2), 5), (("b_rank",), 9),
       (("b_table",), 2)]
    + [(("b_tile", t), 11) for t in range(TILES)]
    + [(("b_pool",), 5), (("b_stats", 3), 3), (("b_degree",), 4), (("b_norm", 3), 5)]
    + [w for c in range(CONVS) for w in (
        [(("b_cgather", c, j), 3.5) for j in range(HALVES)] + [(("b_conv", c, j), 3) for j in range(HALVES)]
        + [(("b_cnatural", c), 3)])])


def weave(a, b):
    whole_a, whole_b = sum(w for _, w in a), sum(w for _, w in b)
    order, at_a, at_b, a, b = [], 0.0, 0.0, list(a), list(b)
    while a or b:
        if a and (not b or at_a * whole_b <= at_b * whole_a):
            stage, w = a.pop(0)
            at_a += w
        else:
            stage, w = b.pop(0)
            at_b += w
        order.append(stage)
    return order


def turns_of(stage):
    name, rest = stage[0], "_".join(map(str, stage[1:]))
    both = {"a_norm": "ahT", "a_q": "q", "a_k": "k", "a_v": "v", "a_rinv": "rinvT", "a_y": "y",
            "b_norm": "hT" + rest, "b_natural": "nat" + rest, "b_pool": "pool", "b_degree": "deg",
            "b_cnatural": "cnat" + rest}
    if name in both:
        return [f"{both[name]}_{j}" for j in range(HALVES)]
    if name == "b_gather":
        return ["u" + rest]
    if name == "b_gates":
        return [g + rest for g in ("r", "hn", "in", "z")]
    if name == "b_edgeT":
        return [f"edgeT_{t}" for t in range(TILES)]
    if name == "b_rank":
        return [f"rank_{t}_{j}" for t in range(TILES) for j in range(HALVES)]
    if name == "b_cgather":
        return ["cu" + rest]
    if name == "b_conv":
        return ["cy" + rest]
    return []


def turn_table(order):
    return {name: i for i, name in enumerate(n for stage in order for n in turns_of(stage))}


def program(nc, A, out):
    f32, f16, bf16 = mybir.dt.float32, mybir.dt.float16, mybir.dt.bfloat16
    i32, f8 = mybir.dt.int32, mybir.dt.float8e4
    u8 = mybir.dt.uint8
    ALU = mybir.AluOpType
    ACT = mybir.ActivationFunctionType
    AX = mybir.AxisListType

    ctx = ExitStack()
    with ctx:
        def sb(name, shape, dt):
            return ctx.enter_context(nc.sbuf_tensor(name, shape, dt))

        def sem(name):
            s = ctx.enter_context(nc.semaphore(name))
            sems.append(s)
            return s

        sems = []

        ident = sb("ident", [P, P], f32)
        ident16 = sb("ident16", [P, P], f16)
        upto = sb("upto", [P, P], f16)
        ones16 = sb("ones16", [P, P], f16)
        wq, wk, wv, wo = (sb(n, [P, DIM], f32) for n in ("wq", "wk", "wv", "wo"))
        wih = sb("wih", [P, GATES * DIM], f32)
        whh = sb("whh", [P, GATES * DIM], f32)
        wmsgT = sb("wmsgT", [P, LAYERS, DIM], f32)
        wgate = sb("wgate", [P, LAYERS, GATES * DIM], f32)
        wpool = sb("wpool", [P, 2, DIM], f32)
        wroot = sb("wroot", [P, CONVS, DIM], f32)
        wrel = sb("wrel", [P, CONVS, DIM], f32)
        cols = sb("cols", [P, 10], f32)
        BQ, BK, BIH, BHH, BCONV = 0, 1, 2, 5, 8
        rows = sb("rows", [P, 5, DIM], f32)
        BV, BO, GAMMA, BETA, BPOOL = range(5)
        half_b = sb("half_b", [P, 3], f32)
        minus_half = sb("minus_half", [P, TILES], f32)
        ones_row = sb("ones_row", [P, NODES], f16)
        slotnum = sb("slotnum", [P, SLOTS + 1], f32)

        raw = sb("raw", [P, 2, NODES], i32)
        edge = sb("edge", [P, TILES, NODES], f16)
        edge1 = sb("edge1", [P, TILES, NODES], u8)
        ahead1 = sb("ahead1", [P, TILES, NODES], u8)
        barred = sb("barred", [P, TILES, NODES], bf16)
        x = sb("x", [P, TILES, DIM], f32)
        ax = sb("ax", [P, TILES, DIM], f32)
        ah = sb("ah", [P, TILES, DIM], f32)
        ahT = sb("ahT", [P, NODES], f32)
        h = sb("h", [P, TILES, DIM], f32)
        hT = sb("hT", [P, NODES], f32)
        high = sb("high", [P, TILES, DIM], f16)
        low = sb("low", [P, TILES, DIM], f16)
        stats = [sb(f"stats_{w}", [P, TILES, 6], f32) for w in "ab"]
        meanvar = [sb(f"meanvar_{w}", [P, TILES, 2], f32) for w in "ab"]
        rstd = [sb(f"rstd_{w}", [P, TILES], f32) for w in "ab"]
        shift = [sb(f"shift_{w}", [P, TILES], f32) for w in "ab"]
        ignored = sb("ignored", [P, NODES], f16)
        qs = sb("qs", [P, HEADS, NODES], f16)
        ks = sb("ks", [P, HEADS, NODES], f16)
        v = sb("v", [P, TILES, DIM], f32)
        masked = sb("masked", [P, 2, NODES], f32)
        prob = sb("prob", [P, 2, NODES], f32)
        parts = [[masked[:, i, :].bitcast(f16)[:, a * NODES:(a + 1) * NODES] for a in range(2)]
                 for i in range(2)]
        probT = sb("probT", [P, RING, TILES, P], f32)
        negmax = sb("negmax", [P, STEPS], f32)
        rowsum = sb("rowsum", [P, STEPS], f32)
        attU = sb("attU", [P, NODES], f32)
        rinv = sb("rinv", [P, STEPS], f32)
        rwide = sb("rwide", [P, TILES, HEADS, HEAD], f32)
        qk32 = [attU, rwide[:, :, :, :].rearrange("p a b c -> p (a b c)")]
        uT = sb("uT", [P, NODES], f32)
        gates = sb("gates", [P, 8, HALF], f32)
        R, X, Z, N = range(4)
        edgeT = gates[:, :, :].rearrange("p a b -> p (a b)").bitcast(f16)\
            .rearrange("p (t n) -> p t n", t=TILES)
        onehot = sb("onehot", [P, NODES], f16)
        maxrank = sb("maxrank", [P, TILES, HALVES], f32)
        slots_f = sb("slots_f", [P, TILES], f32)
        slots_all = sb("slots_all", [P, TILES], f32)
        first_f = sb("first_f", [1, TILES], f32)
        slots_i = sb("slots_i", [1, TILES], i32)
        first_i = sb("first_i", [1, TILES], i32)
        outdeg = sb("outdeg", [P, TILES], f32)
        maxdeg = sb("maxdeg", [P, 1], f32)
        maxdeg_all = sb("maxdeg_all", [P, 1], f32)
        maxdeg_i = sb("maxdeg_i", [1, 1], i32)
        count = sb("count", [P, NODES], f16)
        degrec = sb("degrec", [P, NODES], f32)

        S = ctx.enter_context(nc.psum_tensor("S", [P, NODES], f32))
        PT = ctx.enter_context(nc.psum_tensor("PT", [P, 2, HALF], f32))
        O = ctx.enter_context(nc.psum_tensor("O", [P, HALF], f32))
        G = ctx.enter_context(nc.psum_tensor("G", [P, NB, HALF], f32))

        const_loaded = sem("const_loaded")
        ident_set = sem("ident_set")
        wgate_made = sem("wgate_made")
        x_loaded = sem("x_loaded")
        raw_loaded = [sem(f"raw_loaded{i}") for i in range(2)]
        edge_ready, edge1_ready, barred_ready = sem("edge_ready"), sem("edge1_ready"), sem("barred_ready")
        outdeg_ready = sem("outdeg_ready")
        maxdeg_ready = sem("maxdeg_ready")
        filled = [sem(f"filled{i}") for i in range(NB)]
        drained = [sem(f"drained{i}") for i in range(NB)]
        stats_ready = [sem(f"stats_ready_{w}") for w in "ab"]
        meanvar_ready = [sem(f"meanvar_ready_{w}") for w in "ab"]
        var_ready = [sem(f"var_ready_{w}") for w in "ab"]
        rstd_ready = [sem(f"rstd_ready_{w}") for w in "ab"]
        shift_ready = [sem(f"shift_ready_{w}") for w in "ab"]
        ah_ready = sem("ah_ready")
        ynorm_ready, gain_step, ax_ready = sem("ynorm_ready"), sem("gain_step"), sem("ax_ready")
        ahead1_ready = sem("ahead1_ready")
        h_ready = sem("h_ready")
        high_ready, low_ready = sem("high_ready"), sem("low_ready")
        hT_ready = sem("hT_ready")
        qk32_ready = sem("qk32_ready")
        part_high = sem("part_high")
        stacked = sem("stacked")
        scores_ready, masked_ready, probs_ready = sem("scores_ready"), sem("masked_ready"), sem("probs_ready")
        turned = [sem(f"turned{i}") for i in range(2)]
        probT_ready = [sem(f"probT_ready{i}") for i in range(2)]
        summed, sum_kept = sem("summed"), sem("sum_kept")
        rwide_ready = sem("rwide_ready")
        att_ready = sem("att_ready")
        act_gate = sem("act_gate")
        dve_gate = sem("dve_gate")
        edgeT_ready, rank_ready, slots_summed, slots_known, table_ready = (
            sem("edgeT_ready"), sem("rank_ready"), sem("slots_summed"), sem("slots_known"), sem("table_ready"))
        limit_step, limited = sem("limit_step"), sem("limited")
        onehot_ready = [sem(f"onehot_ready{i}") for i in range(HALVES)]
        pooled = [sem(f"pooled{i}") for i in range(HALVES)]
        picked = [sem(f"picked{i}") for i in range(HALVES)]
        elu_dve, elu_act = sem("elu_dve"), sem("elu_act")
        stored = sem("stored")
        dve_small = sem("dve_small")

        with nc.Block() as block:
            LOADS = [(wq, A["wqT"]), (wk, A["wkT"]), (wv, A["wvT"]), (wo, A["woT"]), (wih, A["wihT"]),
                     (whh, A["whhT"]), (wmsgT, A["wmsgT"]), (wpool, A["wpool"]), (wroot, A["wroot"]),
                     (wrel, A["wrel"]), (cols, A["cols"]), (rows, A["rows"])]

            @block.sync
            def _(sp):
                for dst, src in LOADS:
                    sp.dma_start(dst[tuple([slice(None)] * len(dst.shape))], src).then_inc(const_loaded, 16)

            @block.gpsimd
            def _(pool):
                nc.gpsimd.memset(ident[:, :], 0.0).then_inc(ident_set, 1)
                nc.gpsimd.memset(ident16[:, :], 0.0).then_inc(ident_set, 1)
                nc.gpsimd.memset(upto[:, :], 0.0).then_inc(ident_set, 1)
                nc.gpsimd.memset(ones16[:, :], 1.0)
                nc.gpsimd.memset(minus_half[:, :], -0.5)
                nc.gpsimd.memset(ones_row[:, :], 1.0)
                for k in range(SLOTS + 1):
                    nc.gpsimd.memset(slotnum[:, k:k + 1], float(k + 1))
                pool.wait_ge(ident_set, 3)
                for m in (ident, ident16):
                    nc.gpsimd.affine_select(out=m[:, :], in_=m[:, :], compare_op=ALU.not_equal, fill=1.0,
                                            base=0, pattern=[[-1, P]], channel_multiplier=1).then_inc(ident_set, 1)
                nc.gpsimd.affine_select(out=upto[:, :], in_=upto[:, :], compare_op=ALU.is_gt, fill=1.0,
                                        base=0, pattern=[[-1, P]], channel_multiplier=1).then_inc(ident_set, 1)

            @block.tensor
            def _(pe):
                pe.wait_ge(const_loaded, 16 * len(LOADS))
                for layer in range(LAYERS):
                    nc.tensor.matmul(G[:, layer, 0:GATES * DIM], wmsgT[:, layer, :], wih[:, :],
                                     start=True, stop=True).then_inc(wgate_made, 1)

            @block.vector
            def _(dve):
                dve.wait_ge(const_loaded, 16 * len(LOADS))
                nc.vector.tensor_scalar(cols[:, BQ:BQ + 1], cols[:, BQ:BQ + 1], HEAD ** -0.5, None, op0=ALU.mult)
                nc.vector.tensor_tensor(half_b[:, 0:2], cols[:, BIH:BIH + 2], cols[:, BHH:BHH + 2],
                                        op=ALU.add).then_inc(dve_small, 1)
                dve.wait_ge(dve_small, 1)
                nc.vector.tensor_scalar(half_b[:, 0:2], half_b[:, 0:2], 0.5, None, op0=ALU.mult)
                nc.vector.tensor_scalar(half_b[:, 2:3], cols[:, BHH + 2:BHH + 3], 0.5, None, op0=ALU.mult)
                for layer in range(LAYERS):
                    dve.wait_ge(wgate_made, layer + 1)
                    nc.vector.tensor_copy(wgate[:, layer, :], G[:, layer, 0:GATES * DIM])

        nc.all_engine_barrier(sems_to_clear=range(sems[0].num, sems[-1].num + 1))

        def stages(block, ahead, graph):
            ORDER = weave(ATTENTION if ahead is not None else [], OTHERS if graph is not None else [])
            TURN = turn_table(ORDER)

            def halves(j):
                return slice(j * HALF, (j + 1) * HALF), slice(j * PER_HALF, (j + 1) * PER_HALF)

            def in_tiles(bank):
                return bank.rearrange("p (t c) -> p t c", c=DIM)

            def wait_filled(eng, name):
                i = TURN[name]
                eng.wait_ge(filled[i % NB], i // NB + 1)
                return G[:, i % NB, :]

            def wait_drained(eng, *names):
                for name in names:
                    i = TURN[name]
                    eng.wait_ge(drained[i % NB], i // NB + 1)

            def is_drained(ins, name):
                ins.then_inc(drained[TURN[name] % NB], 1)

            @block.sync
            def _(sp):
                if graph is not None:
                    sp.dma_start(edge1[:, :, :], ahead1[:, :, :]).then_inc(edge1_ready, 16)
                if ahead is not None:
                    sp.dma_start(ax[:, :, :], A["x"][bass.ds(ahead, 1), :, :]
                                 .rearrange("o (t p) c -> p (o t) c", p=P)).then_inc(x_loaded, 16)

                    def load_tile(t):
                        if t >= 2:
                            sp.wait_ge(ahead1_ready, t - 1)
                            sp.wait_ge(barred_ready, t - 1)
                        sp.dma_start(raw[:, t % 2, :], A["adj"][bass.ds(ahead, 1), t * P:(t + 1) * P, :]
                                     .rearrange("o p m -> p (o m)")).then_inc(raw_loaded[t % 2], 16)

                    load_tile(0)
                    load_tile(1)
                    for i, dst in enumerate((qs, ks)):
                        wait_drained(sp, *(f"{'qk'[i]}_{j}" for j in range(HALVES)))
                        for rows_, part in enumerate(((0, 1, 0, 1), (0, 0, 1, 1))[i]):
                            for hd in range(HEADS):
                                sp.dma_start(dst[HEAD * rows_:HEAD * (rows_ + 1), hd, :],
                                             parts[i][part][HEAD * hd:HEAD * (hd + 1), :]).then_inc(stacked, 16)
                    for t in range(2, TILES):
                        load_tile(t)
                if graph is not None:
                    wait_drained(sp, *(f"cnat{CONVS - 1}_{j}" for j in range(HALVES)))
                    sp.dma_start(out[bass.ds(graph, 1), :, :].rearrange("o (t p) c -> p (o t) c", p=P),
                                 h[:, :, :]).then_inc(stored, 16)
                    sp.wait_ge(stored, 16)

            @block.gpsimd
            def _(pool):
                def rstd_of(w, n):
                    pool.wait_ge(meanvar_ready[w], TILES * (n + 1))
                    nc.gpsimd.tensor_scalar(rstd[w][:, :], meanvar[w][:, :, 1], EPS, None,
                                            op0=ALU.add).then_inc(var_ready[w], 1)
                    pool.wait_ge(var_ready[w], n + 1)
                    nc.gpsimd.tensor_tensor(rstd[w][:, :], rstd[w][:, :], minus_half[:, :],
                                            op=ALU.pow).then_inc(rstd_ready[w], 1)

                def masks_ahead():
                    if graph is not None:
                        pool.wait_ge(edge_ready, TILES)
                        pool.wait_ge(edge1_ready, 16)
                    for t in range(TILES):
                        pool.wait_ge(raw_loaded[t % 2], 16 * (t // 2 + 1))
                        nc.gpsimd.tensor_scalar(barred[:, t, :], raw[:, t % 2, :], 0.0, -BIG,
                                                op0=ALU.is_equal, op1=ALU.mult).then_inc(barred_ready, 1)
                        nc.gpsimd.tensor_scalar(ahead1[:, t, :], raw[:, t % 2, :], 1.0, F8_ONE,
                                                op0=ALU.is_equal, op1=ALU.mult).then_inc(ahead1_ready, 1)

                for stage in ORDER:
                    if stage[0] == "b_stats":
                        rstd_of(1, stage[1] - 1)
                    elif stage[0] == "a_stats":
                        rstd_of(0, stage[1])
                    elif stage == ("a_norm",):
                        masks_ahead()
                    elif stage == ("b_limit",):
                        pool.wait_ge(outdeg_ready, TILES + 1)
                        nc.gpsimd.partition_all_reduce(maxdeg_all[:, :], maxdeg[:, :], P,
                                                       bass.bass_isa.ReduceOp.max).then_inc(maxdeg_ready, 1)
                    elif stage == ("b_rank",):
                        pool.wait_ge(slots_summed, 1)
                        nc.gpsimd.partition_all_reduce(slots_all[:, :], slots_f[:, :], P,
                                                       bass.bass_isa.ReduceOp.max).then_inc(slots_known, 1)
                    elif stage == ("a_gain",):
                        pool.wait_ge(ynorm_ready, TILES)
                        for step, (row, op) in enumerate(((GAMMA, ALU.mult), (BETA, ALU.add))):
                            if step:
                                pool.wait_ge(gain_step, step)
                            nc.gpsimd.tensor_tensor(ah[:, :, :], ah[:, :, :],
                                                    rows[:, row:row + 1, :].to_broadcast([P, TILES, DIM]),
                                                    op=op).then_inc(gain_step, 1)

            @block.scalar
            def _(act):
                def affine(w, n, dst, src, func, done):
                    act.wait_ge(shift_ready[w], n + 1)
                    for t in range(TILES):
                        nc.scalar.activation(dst[:, t, :], src[:, t, :], func, scale=rstd[w][:, t:t + 1],
                                             bias=shift[w][:, t:t + 1]).then_inc(done, 1)

                def to_T(name, dst):
                    for j in range(HALVES):
                        bank = wait_filled(act, f"{name}_{j}")
                        is_drained(nc.scalar.activation(dst[:, halves(j)[0]], bank, ACT.Copy), f"{name}_{j}")

                def a_norm():
                    affine(0, 0, ah, ax, ACT.Relu, ah_ready)
                    to_T("ahT", ahT)

                def a_part(i):
                    for j in range(HALVES):
                        act.wait_ge(qk32_ready, HALVES * i + j + 1)
                        nc.scalar.activation(parts[i][0][:, halves(j)[0]], qk32[i][:, halves(j)[0]],
                                             ACT.Copy).then_inc(part_high, 1)

                def a_step(s):
                    if 1 <= s <= STEPS:
                        for j in range(2):
                            act.wait_ge(turned[j], s)
                            if s > RING:
                                act.wait_ge(summed, (s - 1 - RING) // HEADS + 1)
                            nc.scalar.activation(probT[:, (s - 1) % RING, j * PER_HALF:(j + 1) * PER_HALF, :],
                                                 in_tiles(PT[:, j, :]), ACT.Copy).then_inc(probT_ready[j], 1)
                    if s < STEPS:
                        act.wait_ge(masked_ready, s + 1)
                        nc.scalar.activation(prob[:, s % 2, :], masked[:, s % 2, :], ACT.Exp, scale=-1.0,
                                             bias=negmax[:, s:s + 1], accum_out=rowsum[:, s:s + 1])\
                            .then_inc(probs_ready, 1)

                def b_masks():
                    for t in range(TILES):
                        act.wait_ge(edge_ready, t + 1)
                        if t:
                            act.wait_ge(outdeg_ready, t)
                        nc.scalar.activation(ignored[:, :], edge[:, t, :], ACT.Copy,
                                             accum_out=outdeg[:, t:t + 1]).then_inc(outdeg_ready, 1)

                def b_norm(n):
                    affine(1, n - 1, h, x, ACT.Relu, h_ready)
                    act.wait_ge(h_ready, TILES * n)
                    nc.scalar.activation(high[:, :, :], h[:, :, :], ACT.Copy).then_inc(high_ready, 1)
                    to_T(f"hT{n}", hT)

                def b_gather(layer, j):
                    bank = wait_filled(act, f"u{layer}_{j}")
                    is_drained(nc.scalar.activation(uT[:, halves(j)[0]], bank, ACT.Copy), f"u{layer}_{j}")

                def b_gates(layer, j):
                    g = 4 * j
                    for name, place, func, b_ in (("r", R, ACT.Tanh, 0), ("hn", X, ACT.Identity, 2),
                                                  ("z", Z, ACT.Tanh, 1)):
                        bank = wait_filled(act, f"{name}{layer}_{j}")
                        is_drained(nc.scalar.activation(gates[:, g + place, :], bank, func, scale=0.5,
                                                        bias=half_b[:, b_:b_ + 1]), f"{name}{layer}_{j}")
                    wait_drained(act, f"in{layer}_{j}")
                    nc.scalar.activation(gates[:, g + N, :], gates[:, g + X, :], ACT.Tanh,
                                         bias=cols[:, BIH + 2:BIH + 3]).then_inc(act_gate, 1)

                def high_of(name):
                    for j in range(HALVES):
                        nc.scalar.activation(high[:, halves(j)[1], :], in_tiles(wait_filled(act, f"{name}_{j}")),
                                             ACT.Copy).then_inc(high_ready, 1)

                def b_edgeT():
                    for t in range(TILES):
                        bank = wait_filled(act, f"edgeT_{t}")
                        is_drained(nc.scalar.activation(edgeT[:, t, :], bank.bitcast(f16), ACT.Copy), f"edgeT_{t}")

                def b_conv(c, j):
                    act.wait_ge(elu_dve, (c * HALVES + j) * 2 + 1)
                    nc.scalar.activation(gates[:, 2 * j, :], gates[:, 2 * j, :], ACT.Exp).then_inc(elu_act, 1)

                for stage in ORDER:
                    name, args = stage[0], stage[1:]
                    if name == "a_norm":
                        a_norm()
                    elif name in ("a_q", "a_k"):
                        a_part("qk".index(name[2]))
                    elif name == "a_step":
                        a_step(*args)
                    elif name == "a_ynorm":
                        affine(0, 1, ah, ah, ACT.Identity, ynorm_ready)
                    elif name == "b_masks":
                        b_masks()
                    elif name == "b_norm":
                        b_norm(*args)
                    elif name == "b_gather":
                        b_gather(*args)
                    elif name == "b_gates":
                        b_gates(*args)
                    elif name == "b_natural" and args[0] < LAYERS - 1:
                        high_of(f"nat{args[0]}")
                    elif name == "b_edgeT":
                        b_edgeT()
                    elif name == "b_conv":
                        b_conv(*args)
                    elif name == "b_cnatural" and args[0] < CONVS - 1:
                        high_of(f"cnat{args[0]}")

            @block.tensor
            def _(pe):
                def fill(name):
                    i = TURN[name]
                    if i >= NB:
                        pe.wait_ge(drained[i % NB], i // NB)
                    return G[:, i % NB, :]

                def is_full(ins, name):
                    ins.then_inc(filled[TURN[name] % NB], 1)

                def turn_half(name, j, src):
                    bank = fill(name)
                    for t in range(PER_HALF):
                        last = nc.tensor.transpose(bank[:, t * P:(t + 1) * P], src(j * PER_HALF + t), ident[:, :])
                    is_full(last, name)

                def in_T(src):
                    return lambda t: src[:, t * P:(t + 1) * P]

                def gather(name, j, mask):
                    bank = fill(name)
                    for t in range(TILES):
                        for part in (high, low):
                            last = nc.tensor.matmul(bank, part[:, t, :], mask[:, t, halves(j)[0]],
                                                    start=(t == 0 and part is high),
                                                    stop=(t == TILES - 1 and part is low))
                    is_full(last, name)

                def a_norm():
                    for j in range(HALVES):
                        pe.wait_ge(ah_ready, PER_HALF * (j + 1))
                        turn_half(f"ahT_{j}", j, lambda t: ah[:, t, :])

                def a_part(name, w):
                    for j in range(HALVES):
                        wait_drained(pe, f"ahT_{j}")
                        bank = fill(f"{name}_{j}")
                        is_full(nc.tensor.matmul(bank, w[:, :], ahT[:, halves(j)[0]], start=True, stop=True),
                                f"{name}_{j}")

                def a_v():
                    for j in range(HALVES):
                        bank = fill(f"v_{j}")
                        for t in range(PER_HALF):
                            last = nc.tensor.matmul(bank[:, t * P:(t + 1) * P], in_T(ahT)(j * PER_HALF + t), wv[:, :],
                                                    start=True, stop=True)
                        is_full(last, f"v_{j}")

                def scores(s):
                    t, hd = s // HEADS, s % HEADS
                    if s == 0:
                        pe.wait_ge(stacked, 16 * 2 * 4 * HEADS)
                    else:
                        pe.wait_ge(masked_ready, s)
                    for j in range(HALVES):
                        last = nc.tensor.matmul(S[:, halves(j)[0]], qs[:, hd, t * P:(t + 1) * P],
                                                ks[:, hd, halves(j)[0]], start=True, stop=True)
                    last.then_inc(scores_ready, 1)

                def turn_probs(s):
                    pe.wait_ge(probs_ready, s + 1)
                    for j in range(2):
                        if s:
                            pe.wait_ge(probT_ready[j], s)
                        for t in range(PER_HALF):
                            m = j * PER_HALF + t
                            last = nc.tensor.transpose(PT[:, j, t * P:(t + 1) * P],
                                                       prob[:, s % 2, m * P:(m + 1) * P], ident[:, :])
                        last.then_inc(turned[j], 1)

                def weigh(t):
                    if t == 0:
                        wait_drained(pe, "v_0", "v_1")
                    else:
                        pe.wait_ge(sum_kept, t)
                    for j in range(2):
                        pe.wait_ge(probT_ready[j], HEADS * (t + 1))
                    for m in range(TILES):
                        for hd in range(HEADS):
                            last = nc.tensor.matmul(O[HEAD * hd:HEAD * (hd + 1), 0:P],
                                                    v[:, m, HEAD * hd:HEAD * (hd + 1)],
                                                    probT[:, (t * HEADS + hd) % RING, m, :],
                                                    start=(m == 0), stop=(m == TILES - 1))
                    last.then_inc(summed, 1)

                def a_step(s):
                    if s < STEPS:
                        scores(s)
                    if 1 <= s <= STEPS:
                        turn_probs(s - 1)
                    if s > HEADS and s % HEADS == 1:
                        weigh(s // HEADS - 1)

                def a_rinv():
                    pe.wait_ge(rwide_ready, 1)
                    for j in range(HALVES):
                        turn_half(f"rinvT_{j}", j, lambda t: rwide[:, t, :, :].rearrange("p a b -> p (a b)"))

                def a_y():
                    for j in range(HALVES):
                        pe.wait_ge(att_ready, j + 1)
                        bank = fill(f"y_{j}")
                        for t in range(PER_HALF):
                            last = nc.tensor.matmul(bank[:, t * P:(t + 1) * P], in_T(attU)(j * PER_HALF + t), wo[:, :],
                                                    start=True, stop=True)
                        is_full(last, f"y_{j}")

                def b_norm(n):
                    for j in range(HALVES):
                        pe.wait_ge(h_ready, TILES * (n - 1) + PER_HALF * (j + 1))
                        turn_half(f"hT{n}_{j}", j, lambda t: h[:, t, :])

                def b_gather(layer, j):
                    if layer == 0:
                        pe.wait_ge(low_ready, 1)
                        pe.wait_ge(edge_ready, TILES)
                    else:
                        wait_drained(pe, f"nat{layer - 1}_0", f"nat{layer - 1}_1")
                    gather(f"u{layer}_{j}", j, edge)

                def b_gates(layer, j):
                    half = halves(j)[0]
                    wait_drained(pe, f"u{layer}_{j}")
                    if layer == 0:
                        wait_drained(pe, f"hT1_{j}")

                    def gate(name, g, *sides):
                        bank = fill(f"{name}{layer}_{j}")
                        for k, (w, src) in enumerate(sides):
                            last = nc.tensor.matmul(bank, w[:, g * DIM:(g + 1) * DIM], src[:, half],
                                                    start=(k == 0), stop=(k == len(sides) - 1))
                        is_full(last, f"{name}{layer}_{j}")

                    wu = wgate[:, layer, :]
                    gate("r", 0, (wu, uT), (whh, hT))
                    gate("hn", 2, (whh, hT))
                    gate("in", 2, (wu, uT))
                    gate("z", 1, (wu, uT), (whh, hT))

                def b_natural(layer):
                    for j in range(HALVES):
                        pe.wait_ge(dve_gate, (layer * HALVES + j + 1) * 4)
                        turn_half(f"nat{layer}_{j}", j, in_T(hT))

                def b_edgeT():
                    pe.wait_ge(limited, 1)
                    for t in range(TILES):
                        bank = fill(f"edgeT_{t}").bitcast(f16)
                        for n in range(TILES):
                            last = nc.tensor.transpose(bank[:, n * P:(n + 1) * P], edge[:, n, t * P:(t + 1) * P],
                                                       ident16[:, :])
                        is_full(last, f"edgeT_{t}")

                def b_rank():
                    for t in range(TILES):
                        wait_drained(pe, f"edgeT_{t}")
                        for j in range(HALVES):
                            bank = fill(f"rank_{t}_{j}")
                            is_full(nc.tensor.matmul(bank, upto[:, :], edgeT[:, t, halves(j)[0]],
                                                     start=True, stop=True), f"rank_{t}_{j}")

                def b_table():
                    for bank in range(HALVES):
                        used = sum(1 for i in range(before_slots) if i % NB == bank)
                        pe.wait_ge(drained[bank], used)
                    pe.wait_ge(table_ready, 2)
                    pe.wait_ge(low_ready, 2)

                def b_tile(t):
                    n_slots = pe.value_load(slots_i[0:1, t:t + 1], min_val=1, max_val=SLOTS)
                    first = pe.value_load(first_i[0:1, t:t + 1], min_val=t, max_val=SLOTS * TILES)
                    with pe.Fori(0, n_slots) as k:
                        for j in range(HALVES):
                            pe.wait_ge(onehot_ready[j], first + k + (t + 1))
                            pe.wait_ge(pooled[j], first + (k + 1))
                            nc.tensor.matmul(G[:, j, :], high[:, t, :], onehot[:, halves(j)[0]],
                                             start=True, stop=False)
                            nc.tensor.matmul(G[:, j, :], low[:, t, :], onehot[:, halves(j)[0]],
                                             start=False, stop=True).then_inc(picked[j], 1)
                    if t == TILES - 1:
                        for j in range(HALVES):
                            pe.wait_ge(pooled[j], first + n_slots + 1)

                def b_pool():
                    wait_drained(pe, "hT2_0", "hT2_1")
                    for j in range(HALVES):
                        bank = fill(f"pool_{j}")
                        for t in range(PER_HALF):
                            o, n = bank[:, t * P:(t + 1) * P], j * PER_HALF + t
                            nc.tensor.matmul(o, in_T(hT)(n), wpool[:, 0, :], start=True, stop=False)
                            last = nc.tensor.matmul(o, in_T(uT)(n), wpool[:, 1, :], start=False, stop=True)
                        is_full(last, f"pool_{j}")

                def b_degree():
                    pe.wait_ge(edge1_ready, 16)
                    for j in range(HALVES):
                        bank = fill(f"deg_{j}")
                        for t in range(TILES):
                            last = nc.tensor.matmul(bank, ones16[:, :], edge1[:, t, halves(j)[0]].bitcast(f8),
                                                    start=(t == 0), stop=(t == TILES - 1))
                        is_full(last, f"deg_{j}")

                def b_cgather(c, j):
                    if c == 0:
                        pe.wait_ge(low_ready, 3)
                    else:
                        wait_drained(pe, f"cnat{c - 1}_0", f"cnat{c - 1}_1")
                    gather(f"cu{c}_{j}", j, edge1[:, :, :].bitcast(f8))

                def b_conv(c, j):
                    if c == 0:
                        wait_drained(pe, f"hT3_{j}")
                    wait_drained(pe, f"cu{c}_{j}")
                    bank, half = fill(f"cy{c}_{j}"), halves(j)[0]
                    nc.tensor.matmul(bank, wroot[:, c, :], hT[:, half], start=True, stop=False)
                    is_full(nc.tensor.matmul(bank, wrel[:, c, :], uT[:, half], start=False, stop=True), f"cy{c}_{j}")

                def b_cnatural(c):
                    for j in range(HALVES):
                        pe.wait_ge(elu_dve, (c * HALVES + j) * 2 + 2)
                        turn_half(f"cnat{c}_{j}", j, in_T(hT))

                before_slots = 0
                for stage in ORDER:
                    if stage == ("b_table",):
                        break
                    before_slots += len(turns_of(stage))
                for stage in ORDER:
                    name, args = stage[0], stage[1:]
                    if name == "a_norm":
                        a_norm()
                    elif name == "a_q":
                        a_part("q", wq)
                    elif name == "a_k":
                        a_part("k", wk)
                    elif name == "a_v":
                        a_v()
                    elif name == "a_step":
                        a_step(*args)
                    elif name == "a_rinv":
                        a_rinv()
                    elif name == "a_y":
                        a_y()
                    elif name == "b_norm":
                        b_norm(*args)
                    elif name == "b_gather":
                        b_gather(*args)
                    elif name == "b_gates":
                        b_gates(*args)
                    elif name == "b_natural":
                        b_natural(*args)
                    elif name == "b_edgeT":
                        b_edgeT()
                    elif name == "b_rank":
                        b_rank()
                    elif name == "b_table":
                        b_table()
                    elif name == "b_tile":
                        b_tile(*args)
                    elif name == "b_pool":
                        b_pool()
                    elif name == "b_degree":
                        b_degree()
                    elif name == "b_cgather":
                        b_cgather(*args)
                    elif name == "b_conv":
                        b_conv(*args)
                    elif name == "b_cnatural":
                        b_cnatural(*args)

            @block.vector
            def _(dve):
                small = [0]

                def link(ins):
                    small[0] += 1
                    ins.then_inc(dve_small, 1)
                    dve.wait_ge(dve_small, small[0])

                def mean_and_var(w, n, src):
                    for t in range(TILES):
                        nc.vector.bn_stats(stats[w][:, t, :], src[:, t, :]).then_inc(stats_ready[w], 1)
                    for t in range(TILES):
                        dve.wait_ge(stats_ready[w], TILES * n + t + 1)
                        nc.vector.bn_aggr(meanvar[w][:, t, :], stats[w][:, t, :]).then_inc(meanvar_ready[w], 1)

                def shift_of(w, n):
                    dve.wait_ge(rstd_ready[w], n + 1)
                    nc.vector.scalar_tensor_tensor(shift[w][:, :], meanvar[w][:, :, 0], -1.0, rstd[w][:, :],
                                                   op0=ALU.mult, op1=ALU.mult).then_inc(shift_ready[w], 1)

                def add_row(name, dst, row):
                    for j in range(HALVES):
                        bank = wait_filled(dve, f"{name}_{j}")
                        is_drained(nc.vector.tensor_tensor(
                            dst[:, halves(j)[1], :], in_tiles(bank),
                            rows[:, row:row + 1, :].to_broadcast([P, PER_HALF, DIM]), op=ALU.add), f"{name}_{j}")

                def a_stats(n):
                    if n == 0:
                        dve.wait_ge(x_loaded, 16)
                    else:
                        wait_drained(dve, "y_0", "y_1")
                    mean_and_var(0, n, (ax, ah)[n])

                def a_part(i):
                    for j in range(HALVES):
                        half, name = halves(j)[0], f"{'qk'[i]}_{j}"
                        nc.vector.tensor_scalar(qk32[i][:, half], wait_filled(dve, name), (HEAD ** -0.5, 1.0)[i],
                                                cols[:, BQ + i:BQ + i + 1], op0=ALU.mult,
                                                op1=ALU.add).then_inc(qk32_ready, 1)
                        dve.wait_ge(part_high, HALVES * i + j + 1)
                        is_drained(nc.vector.tensor_tensor(parts[i][1][:, half], qk32[i][:, half], parts[i][0][:, half],
                                                           op=ALU.subtract), name)

                def a_step(s):
                    if s < STEPS:
                        dve.wait_ge(scores_ready, s + 1)
                        dve.wait_ge(barred_ready, s // HEADS + 1)
                        if s >= 2:
                            dve.wait_ge(probs_ready, s - 1)
                        nc.vector.tensor_tensor_reduce(out=masked[:, s % 2, :], in0=S[:, :],
                                                       in1=barred[:, s // HEADS, :], scale=-1.0, scalar=3.0e38,
                                                       op0=ALU.add, op1=ALU.min,
                                                       accum_out=negmax[:, s:s + 1]).then_inc(masked_ready, 1)
                    if s > HEADS and s % HEADS == 2:
                        keep_sum(s // HEADS - 1)

                def keep_sum(t):
                    dve.wait_ge(summed, t + 1)
                    nc.vector.tensor_copy(attU[:, t * P:(t + 1) * P], O[:, 0:P]).then_inc(sum_kept, 1)

                def a_rinv():
                    keep_sum(TILES - 1)
                    dve.wait_ge(probs_ready, STEPS)
                    link(nc.vector.reciprocal(rinv[:, :], rowsum[:, :]))
                    nc.vector.tensor_copy(rwide[:, :, :, :].rearrange("p a b c -> p (a b) c"),
                                          rinv[:, :].unsqueeze(2).to_broadcast([P, STEPS, HEAD])).then_inc(rwide_ready, 1)
                    dve.wait_ge(sum_kept, TILES)
                    for j in range(HALVES):
                        half, name = halves(j)[0], f"rinvT_{j}"
                        nc.vector.tensor_tensor(attU[:, half], attU[:, half], wait_filled(dve, name),
                                                op=ALU.mult).then_inc(att_ready, 1)
                        dve.wait_ge(att_ready, j + 1)
                        dve.sem_inc(drained[TURN[name] % NB], 1)

                def a_end():
                    dve.wait_ge(gain_step, 2)
                    nc.vector.tensor_tensor(x[:, :, :], ax[:, :, :], ah[:, :, :], op=ALU.add).then_inc(ax_ready, 1)

                def b_masks():
                    for t in range(TILES):
                        nc.vector.tensor_scalar(edge[:, t, :], barred[:, t, :], 0.0, None,
                                                op0=ALU.is_equal).then_inc(edge_ready, 1)

                def b_norm(n):
                    shift_of(1, n - 1)
                    dve.wait_ge(high_ready, {1: 1, 2: 2 + HALVES * (LAYERS - 1), 3: 3 + HALVES * (LAYERS - 1)}[n])
                    nc.vector.tensor_tensor(low[:, :, :], h[:, :, :], high[:, :, :],
                                            op=ALU.subtract).then_inc(low_ready, 1)

                def b_gates(layer, j):
                    g, half, step = 4 * j, halves(j)[0], (layer * HALVES + j) * 4
                    wait_drained(dve, f"r{layer}_{j}", f"hn{layer}_{j}")
                    nc.vector.scalar_tensor_tensor(gates[:, g + X, :], gates[:, g + R, :], 1.0, gates[:, g + X, :],
                                                   op0=ALU.add, op1=ALU.mult).then_inc(dve_gate, 1)
                    dve.wait_ge(dve_gate, step + 1)
                    is_drained(nc.vector.tensor_tensor(gates[:, g + X, :], gates[:, g + X, :],
                                                       wait_filled(dve, f"in{layer}_{j}"), op=ALU.add),
                               f"in{layer}_{j}")
                    dve.wait_ge(act_gate, layer * HALVES + j + 1)
                    nc.vector.tensor_tensor(gates[:, g + R, :], hT[:, half], gates[:, g + N, :],
                                            op=ALU.subtract).then_inc(dve_gate, 1)
                    dve.wait_ge(dve_gate, step + 2)
                    nc.vector.scalar_tensor_tensor(gates[:, g + R, :], gates[:, g + Z, :], 1.0, gates[:, g + R, :],
                                                   op0=ALU.add, op1=ALU.mult).then_inc(dve_gate, 1)
                    dve.wait_ge(dve_gate, step + 3)
                    nc.vector.scalar_tensor_tensor(hT[:, half], gates[:, g + R, :], 0.5, gates[:, g + N, :],
                                                   op0=ALU.mult, op1=ALU.add).then_inc(dve_gate, 1)

                def low_of(name, high_count):
                    for j in range(HALVES):
                        bank, tiles = in_tiles(wait_filled(dve, f"{name}_{j}")), halves(j)[1]
                        dve.wait_ge(high_ready, high_count + j)
                        is_drained(nc.vector.tensor_tensor(low[:, tiles, :], bank, high[:, tiles, :],
                                                           op=ALU.subtract), f"{name}_{j}")

                def add_to(dst, name):
                    for j in range(HALVES):
                        bank, tiles = in_tiles(wait_filled(dve, f"{name}_{j}")), halves(j)[1]
                        is_drained(nc.vector.tensor_tensor(dst[:, tiles, :], x[:, tiles, :], bank, op=ALU.add),
                                   f"{name}_{j}")
                    wait_drained(dve, f"{name}_0", f"{name}_1")

                def b_limit():
                    last = f"u{LAYERS - 1}"
                    wait_filled(dve, f"{last}_0")
                    wait_filled(dve, f"{last}_1")
                    dve.wait_ge(outdeg_ready, TILES)
                    nc.vector.tensor_reduce(maxdeg[:, :], outdeg[:, :], axis=AX.X, op=ALU.max).then_inc(outdeg_ready, 1)
                    dve.wait_ge(maxdeg_ready, 1)
                    link(nc.vector.tensor_copy(maxdeg_i[:, :], maxdeg_all[0:1, :]))
                    most = dve.value_load(maxdeg_i[0:1, 0:1], min_val=0, max_val=NODES)
                    with dve.If(most > SLOTS):
                        for t in range(TILES):
                            nc.vector.tensor_tensor_scan(count[:, :], ones_row[:, :], edge[:, t, :], 0.0, ALU.mult,
                                                         ALU.add).then_inc(limit_step, 1)
                            dve.wait_ge(limit_step, 2 * t + 1)
                            nc.vector.scalar_tensor_tensor(edge[:, t, :], count[:, :], float(SLOTS), edge[:, t, :],
                                                           op0=ALU.is_le, op1=ALU.mult).then_inc(limit_step, 1)
                            dve.wait_ge(limit_step, 2 * t + 2)
                    dve.sem_inc(limited, 1)

                def b_rank():
                    for t in range(TILES):
                        for j in range(HALVES):
                            here = edgeT[:, t, halves(j)[0]]
                            is_drained(nc.vector.tensor_tensor_reduce(
                                out=here, in0=wait_filled(dve, f"rank_{t}_{j}"), in1=here, scale=1.0, scalar=0.0,
                                op0=ALU.mult, op1=ALU.max, accum_out=maxrank[:, t, j:j + 1]), f"rank_{t}_{j}")
                    wait_drained(dve, *(f"rank_{t}_{j}" for t in range(TILES) for j in range(HALVES)))
                    nc.vector.tensor_tensor(slots_f[:, :], maxrank[:, :, 0], maxrank[:, :, 1],
                                            op=ALU.max).then_inc(slots_summed, 1)

                def b_table():
                    dve.wait_ge(slots_known, 1)
                    link(nc.vector.tensor_scalar(slots_all[0:1, :], slots_all[0:1, :], 1.0, None, op0=ALU.max))
                    link(nc.vector.tensor_tensor_scan(first_f[:, :], ones_row[0:1, 0:TILES], slots_all[0:1, :], 0.0,
                                                      ALU.mult, ALU.add))
                    nc.vector.tensor_copy(slots_i[:, :], slots_all[0:1, :]).then_inc(table_ready, 1)
                    nc.vector.tensor_tensor(first_i[:, :], first_f[:, :], slots_all[0:1, :],
                                            op=ALU.subtract).then_inc(table_ready, 1)
                    for j in range(HALVES):
                        nc.vector.memset(uT[:, halves(j)[0]], 0.0).then_inc(pooled[j], 1)
                    dve.wait_ge(table_ready, 2)

                def b_tile(t):
                    n_slots = dve.value_load(slots_i[0:1, t:t + 1], min_val=1, max_val=SLOTS)
                    first = dve.value_load(first_i[0:1, t:t + 1], min_val=t, max_val=SLOTS * TILES)
                    for j in range(HALVES):
                        if t:
                            dve.wait_ge(picked[j], first)
                            dve.wait_ge(onehot_ready[j], first + t)
                        nc.vector.tensor_scalar(onehot[:, halves(j)[0]], edgeT[:, t, halves(j)[0]], slotnum[:, 0:1],
                                                None, op0=ALU.is_equal).then_inc(onehot_ready[j], 1)
                    with dve.Fori(0, n_slots) as k:
                        for j in range(HALVES):
                            half = halves(j)[0]
                            dve.wait_ge(picked[j], first + k + 1)
                            dve.wait_ge(onehot_ready[j], first + k + (t + 1))
                            nc.vector.tensor_scalar(onehot[:, half], edgeT[:, t, half],
                                                    slotnum[:, bass.ds(k + 1, 1)], None,
                                                    op0=ALU.is_equal).then_inc(onehot_ready[j], 1)
                            dve.wait_ge(pooled[j], first + (k + 1))
                            nc.vector.tensor_tensor(uT[:, half], uT[:, half], G[:, j, :],
                                                    op=ALU.max).then_inc(pooled[j], 1)

                def b_pool():
                    add_row("pool", h, BPOOL)
                    wait_drained(dve, "pool_0", "pool_1")
                    link(nc.vector.scalar_tensor_tensor(x[:, :, :], h[:, :, :], 0.0, x[:, :, :],
                                                        op0=ALU.max, op1=ALU.add))

                def b_degree():
                    for j in range(HALVES):
                        bank = wait_filled(dve, f"deg_{j}")
                        is_drained(nc.vector.tensor_scalar(degrec[:, halves(j)[0]], bank, 1.0, None, op0=ALU.max),
                                   f"deg_{j}")
                    wait_drained(dve, "deg_0", "deg_1")
                    link(nc.vector.reciprocal(degrec[:, :], degrec[:, :]))

                def b_cgather(c, j):
                    bank, half = wait_filled(dve, f"cu{c}_{j}"), halves(j)[0]
                    is_drained(nc.vector.tensor_tensor(uT[:, half], bank, degrec[:, half], op=ALU.mult), f"cu{c}_{j}")

                def b_conv(c, j):
                    bias, half, name = cols[:, BCONV + c:BCONV + c + 1], halves(j)[0], f"cy{c}_{j}"
                    bank = wait_filled(dve, name)
                    nc.vector.tensor_scalar(gates[:, 2 * j, :], bank, bias, 0.0, op0=ALU.add,
                                            op1=ALU.min).then_inc(elu_dve, 1)
                    is_drained(nc.vector.tensor_scalar(gates[:, 2 * j + 1, :], bank, bias, 0.0, op0=ALU.add,
                                                       op1=ALU.max), name)
                    wait_drained(dve, name)
                    dve.wait_ge(elu_act, c * HALVES + j + 1)
                    nc.vector.scalar_tensor_tensor(hT[:, half], gates[:, 2 * j, :], -1.0, gates[:, 2 * j + 1, :],
                                                   op0=ALU.add, op1=ALU.add).then_inc(elu_dve, 1)

                for stage in ORDER:
                    name, args = stage[0], stage[1:]
                    if name == "a_stats":
                        a_stats(*args)
                    elif name == "a_norm":
                        shift_of(0, 0)
                    elif name in ("a_q", "a_k"):
                        a_part("qk".index(name[2]))
                    elif name == "a_v":
                        add_row("v", v, BV)
                    elif name == "a_step":
                        a_step(*args)
                    elif name == "a_rinv":
                        a_rinv()
                    elif name == "a_y":
                        add_row("y", ah, BO)
                    elif name == "a_ynorm":
                        shift_of(0, 1)
                    elif name == "b_stats":
                        mean_and_var(1, args[0] - 1, x)
                    elif name == "b_masks":
                        b_masks()
                    elif name == "b_norm":
                        b_norm(*args)
                    elif name == "b_gates":
                        b_gates(*args)
                    elif name == "b_natural":
                        if args[0] < LAYERS - 1:
                            low_of(f"nat{args[0]}", 2 + HALVES * args[0])
                        else:
                            add_to(x, f"nat{args[0]}")
                    elif name == "b_limit":
                        b_limit()
                    elif name == "b_rank":
                        b_rank()
                    elif name == "b_table":
                        b_table()
                    elif name == "b_tile":
                        b_tile(*args)
                    elif name == "b_pool":
                        b_pool()
                    elif name == "b_degree":
                        b_degree()
                    elif name == "b_cgather":
                        b_cgather(*args)
                    elif name == "b_conv":
                        b_conv(*args)
                    elif name == "b_cnatural":
                        if args[0] < CONVS - 1:
                            low_of(f"cnat{args[0]}", 4 + HALVES * (LAYERS - 1) + HALVES * args[0])
                        else:
                            add_to(h, f"cnat{args[0]}")
                if ahead is not None:
                    a_end()

        def turn(ahead, graph):
            with nc.Block() as block:
                stages(block, ahead, graph)
            nc.all_engine_barrier(sems_to_clear=range(sems[0].num, sems[-1].num + 1))

        turn(0, None)
        with nc.Fori(0, BATCH - 1) as b:
            turn(b + 1, b)
        turn(None, BATCH - 1)


def kernel(**inputs):
    import numpy as np
    import concourse.bacc as bacc
    from concourse.bass_utils import run_bass_kernel_spmd

    a = {n: np.asarray(v) for n, v in inputs.items()}

    def column_blocks(v):
        return v.reshape(-1, 128).T

    layout = {
        "x": a["x"], "adj": a["adj"],
        "wqT": a["L0_gnn_Wq"].T, "wkT": a["L0_gnn_Wk"].T, "wvT": a["L0_gnn_Wv"].T, "woT": a["L0_gnn_Wo"].T,
        "wihT": a["L1_gnn_w_ih"].T, "whhT": a["L1_gnn_w_hh"].T,
        "wmsgT": a["L1_gnn_weight"].transpose(2, 0, 1),
        "wpool": a["L2_gnn_W"].reshape(2, 128, 128).transpose(1, 0, 2),
        "wroot": np.stack([a["L3_gnn_w_root1"], a["L3_gnn_w_root2"]], 1),
        "wrel": np.stack([a["L3_gnn_w_rel1"][1], a["L3_gnn_w_rel2"][1]], 1),
        "cols": np.concatenate([column_blocks(a[n]) for n in (
            "L0_gnn_bq", "L0_gnn_bk", "L1_gnn_b_ih", "L1_gnn_b_hh", "L3_gnn_b1", "L3_gnn_b2")], 1),
        "rows": np.broadcast_to(np.stack([a[n] for n in (
            "L0_gnn_bv", "L0_gnn_bo", "L0_gnn_gamma", "L0_gnn_beta", "L2_gnn_b")]), (128, 5, 128)),
    }
    nc = bacc.Bacc("TRN2", target_bir_lowering=False, num_devices=1)
    arrays, args = {}, {}
    for name, v in layout.items():
        v = np.ascontiguousarray(v)
        arrays[f"in_{name}_dram"] = v
        args[name] = nc.dram_tensor(f"in_{name}_dram", v.shape, mybir.dt.from_np(v.dtype), kind="ExternalInput").ap()
    out = nc.dram_tensor("out_0_dram", (BATCH, NODES, DIM), mybir.dt.float32, kind="ExternalOutput").ap()
    program(nc, args, out)
    r = run_bass_kernel_spmd(nc, [arrays], core_ids=[0])
    return r.results[0]["out_0_dram"]
```

```python
import concourse.bass as bass
from concourse import mybir
from contextlib import ExitStack

P = 128
BATCH, NODES, DIM = 8, 1024, 128
TILES = NODES // P
HEADS = 4
HEAD = DIM // HEADS
HALF = 512
HALVES = NODES // HALF
PER_HALF = HALF // P
LAYERS = 3
CONVS = 2
GATES = 3
STEPS = TILES * HEADS
RING = 5
SLOTS = 25
FIXED = 6
BIG = 2.0 ** 100
EPS = 1e-5
F8_ONE = 0x38
FIRST_SLOTS = 39
RINGS = {"a": 4, "b": 3}


def slots(first, last):
    return [("b_slot", i) for i in range(first, last)]


def order_of():
    order = [("b_rank", 0), ("b_rank", 1), ("b_stats", 0), ("b_rank", 2), ("b_rank", 3), ("a_stats", 0),
             ("b_rank", 4), ("a_norm", 0), ("b_rank", 5), ("a_q",), ("a_k",), ("b_rank", 6), ("b_rank", 7),
             ("b_norm", 0), ("a_v",), ("b_table",)]
    order += slots(0, 2)
    taken = 2
    for step in range(STEPS + 3):
        upto = 2 + (step + 1) * (FIRST_SLOTS - 2) // (STEPS + 3)
        order += [("a_step", step)] + slots(taken, upto) + [("a_turn", step)]
        taken = upto
    rest = slots(FIRST_SLOTS, TILES * FIXED)
    cuts = [round(i * len(rest) / 9) for i in range(10)]
    rest = [rest[a:b] for a, b in zip(cuts, cuts[1:])]
    order += [("a_rinv",)] + rest[0] + [("a_outdeg", t) for t in range(4)] + [("a_y",)] + rest[1]
    order += [("a_stats", 1)] + [("a_outdeg", t) for t in range(4, TILES)] + rest[2] + [("a_ynorm",)] + rest[3] + rest[4]
    order += [("a_gain",), ("a_stats", 2)] + rest[5] + [("a_norm", 1)] + rest[6] + rest[7] + rest[8]
    order += [("a_gather", 0, 0), ("a_gather", 0, 1), ("b_extra",), ("a_gates", 0, 0), ("b_pool",), ("a_gates", 0, 1),
              ("b_stats", 1), ("b_degree",),
              ("a_natural", 0, 0), ("a_gather", 1, 0), ("a_natural", 0, 1), ("b_norm", 1), ("a_gather", 1, 1),
              ("a_gates", 1, 0), ("b_degrec",), ("b_cgather", 0, 0), ("a_gates", 1, 1), ("b_cgather", 0, 1),
              ("a_natural", 1, 0), ("a_gather", 2, 0), ("b_conv", 0, 0), ("a_natural", 1, 1), ("b_conv", 0, 1),
              ("a_gather", 2, 1), ("a_limit",), ("b_cnatural", 0, 0), ("a_gates", 2, 0), ("b_cnatural", 0, 1),
              ("b_cgather", 1, 0), ("a_gates", 2, 1), ("b_cgather", 1, 1), ("a_natural", 2, 0),
              ("b_conv", 1, 0), ("b_conv", 1, 1), ("a_natural", 2, 1), ("a_edgeT", 0), ("a_edgeT", 1), ("a_edgeT", 2),
              ("b_cnatural", 1, 0), ("b_cnatural", 1, 1)] + [("a_edgeT", t) for t in range(3, TILES)]
    return order


def turns_of(stage):
    name, rest = stage[0], "_".join(map(str, stage[1:]))
    both = {"a_norm": "ahT" + rest, "a_q": "q", "a_k": "k", "a_v": "v", "a_rinv": "rinvT", "a_y": "y",
            "b_norm": "hT" + rest, "b_pool": "pool", "b_degrec": "degrec"}
    if name in both:
        return [f"{both[name]}_{j}" for j in range(HALVES)]
    if name in ("a_gather", "b_cgather"):
        u = "u" if name == "a_gather" else "cu"
        return [f"{u}{stage[1]}_{j}" for j in range(HALVES)] if stage[2] == 0 else []
    if name in ("a_natural", "b_cnatural"):
        return [("nat" if name == "a_natural" else "cnat") + rest]
    if name == "a_gates":
        return [g + rest for g in ("r", "hn", "in", "z")]
    if name == "a_edgeT":
        return ["edgeT_" + rest]
    if name == "b_degree":
        return ["degcol"]
    if name == "b_slot":
        return [f"slot{rest}_{j}" for j in range(HALVES)]
    if name == "b_rank":
        return [f"rank_{rest}_{j}" for j in range(HALVES)]
    if name == "b_conv":
        return ["cy" + rest]
    return []


def turn_table(order):
    table = {}
    for stream in RINGS:
        names = [n for stage in order if stage[0].startswith(stream) for n in turns_of(stage)]
        table.update((name, (stream, i)) for i, name in enumerate(names))
    return table


def program(nc, A, out):
    f32, f16, bf16 = mybir.dt.float32, mybir.dt.float16, mybir.dt.bfloat16
    i32, f8 = mybir.dt.int32, mybir.dt.float8e4
    u8 = mybir.dt.uint8
    ALU = mybir.AluOpType
    ACT = mybir.ActivationFunctionType
    AX = mybir.AxisListType

    ctx = ExitStack()
    with ctx:
        def sb(name, shape, dt):
            return ctx.enter_context(nc.sbuf_tensor(name, shape, dt))

        def sem(name):
            s = ctx.enter_context(nc.semaphore(name))
            sems.append(s)
            return s

        sems = []

        ident = sb("ident", [P, P], f32)
        ident16 = sb("ident16", [P, P], f16)
        upto = sb("upto", [P, P], f16)
        ones16 = sb("ones16", [P, P], f16)
        wq, wk, wv, wo = (sb(n, [P, DIM], f32) for n in ("wq", "wk", "wv", "wo"))
        wih = sb("wih", [P, GATES * DIM], f32)
        whh = sb("whh", [P, GATES * DIM], f32)
        wmsgT = sb("wmsgT", [P, LAYERS, DIM], f32)
        wgate = sb("wgate", [P, LAYERS, GATES * DIM], f32)
        wpool = sb("wpool", [P, 2, DIM], f32)
        wroot = sb("wroot", [P, CONVS, DIM], f32)
        wrel = sb("wrel", [P, CONVS, DIM], f32)
        cols = sb("cols", [P, 10], f32)
        BQ, BK, BIH, BHH, BCONV = 0, 1, 2, 5, 8
        rows = sb("rows", [P, 5, DIM], f32)
        BV, BO, GAMMA, BETA, BPOOL = range(5)
        half_b = sb("half_b", [P, 3], f32)
        minus_half = sb("minus_half", [P, TILES], f32)
        ones_row = sb("ones_row", [P, NODES], f16)
        slotnum = sb("slotnum", [P, SLOTS + 1], f32)

        raw = sb("raw", [P, 2, NODES], i32)
        edge = sb("edge", [P, TILES, NODES], f16)
        barred = edge[:, :, :].rearrange("p t n -> p (t n)").bitcast(bf16)\
            .rearrange("p (t n) -> p t n", t=TILES)
        edge1 = sb("edge1", [P, TILES, NODES], u8)
        ahead1 = sb("ahead1", [P, TILES, NODES], u8)
        x = sb("x", [P, TILES, DIM], f32)
        ax = sb("ax", [P, TILES, DIM], f32)
        ah = sb("ah", [P, TILES, DIM], f32)
        ahT = sb("ahT", [P, NODES], f32)
        h = sb("h", [P, TILES, DIM], f32)
        hT = sb("hT", [P, NODES], f32)
        high = sb("high", [P, TILES, DIM], f16)
        low = sb("low", [P, TILES, DIM], f16)
        ahigh = sb("ahigh", [P, TILES, DIM], f16)
        alow = sb("alow", [P, TILES, DIM], f16)
        stats = [sb(f"stats_{w}", [P, TILES, 6], f32) for w in "ab"]
        meanvar = [sb(f"meanvar_{w}", [P, TILES, 2], f32) for w in "ab"]
        rstd = [sb(f"rstd_{w}", [P, TILES], f32) for w in "ab"]
        shift = [sb(f"shift_{w}", [P, TILES], f32) for w in "ab"]
        ignored = sb("ignored", [P, NODES], f16)
        stack = sb("stack", [P, 2, HEADS, NODES], f16)
        qs, ks = stack[:, 0, :, :], stack[:, 1, :, :]
        v = sb("v", [P, TILES, DIM], f32)
        masked = sb("masked", [P, 2, NODES], f32)
        prob = sb("prob", [P, 2, NODES], f32)
        probT = sb("probT", [P, RING, TILES, P], f32)
        all_parts = probT[:, RING - 2:RING, :, :].rearrange("p a t n -> p (a t n)").bitcast(f16)\
            .rearrange("p (a n) -> p a n", a=4)
        parts = [[all_parts[:, 2 * i + a, :] for a in range(2)] for i in range(2)]
        negmax = sb("negmax", [P, STEPS], f32)
        rowsum = sb("rowsum", [P, STEPS], f32)
        attU = sb("attU", [P, NODES], f32)
        rinv = sb("rinv", [P, STEPS], f32)
        rwide = sb("rwide", [P, TILES, HEADS, HEAD], f32)
        qk32 = [attU, rwide[:, :, :, :].rearrange("p a b c -> p (a b c)")]
        uT = sb("uT", [P, NODES], f32)
        auT = attU
        gates = stack[:, :, :, :].rearrange("p a b c -> p (a b c)").bitcast(f32)\
            .rearrange("p (g n) -> p g n", g=8)
        R, X, Z, N = range(4)
        elu = sb("elu", [P, 4, HALF], f32)
        edgeT = sb("edgeT", [P, TILES, NODES], f16)
        onehot = sb("onehot", [P, 2, NODES], f16)
        maxrank = sb("maxrank", [P, TILES, HALVES], f32)
        slots_f = sb("slots_f", [P, TILES], f32)
        slots_all = sb("slots_all", [P, TILES], f32)
        first_f = sb("first_f", [1, TILES], f32)
        extra_i = sb("extra_i", [1, TILES], i32)
        more_i = sb("more_i", [1, 1], i32)
        first_i = sb("first_i", [1, TILES], i32)
        outdeg = sb("outdeg", [P, TILES], f32)
        maxdeg = sb("maxdeg", [P, 1], f32)
        maxdeg_all = sb("maxdeg_all", [P, 1], f32)
        maxdeg_i = sb("maxdeg_i", [1, 1], i32)
        count = ignored
        deg = sb("deg", [P, TILES], f32)
        degwide = elu[:, 0:2, :].rearrange("p a b -> p (a b)").rearrange("p (t c) -> p t c", t=TILES)
        degrec = sb("degrec", [P, NODES], f32)

        AB = ctx.enter_context(nc.psum_tensor("AB", [P, RINGS["a"], HALF], f32))
        S = AB[:, 0:2, :].rearrange("p a b -> p (a b)")
        PT = AB[:, 2:4, :]
        O = ctx.enter_context(nc.psum_tensor("O", [P, HALF], f32))
        G = ctx.enter_context(nc.psum_tensor("G", [P, RINGS["b"], HALF], f32))

        const_loaded = sem("const_loaded")
        ident_set = sem("ident_set")
        wgate_made = sem("wgate_made")
        x_loaded = sem("x_loaded")
        raw_loaded = [sem(f"raw_loaded{i}") for i in range(2)]
        edge_ready, edge1_ready, barred_ready = sem("edge_ready"), sem("edge1_ready"), sem("barred_ready")
        outdeg_ready = sem("outdeg_ready")
        maxdeg_ready = sem("maxdeg_ready")
        filled = {w: [sem(f"filled_{w}{i}") for i in range(n)] for w, n in RINGS.items()}
        drained = {w: [sem(f"drained_{w}{i}") for i in range(n)] for w, n in RINGS.items()}
        stats_ready = [sem(f"stats_ready_{w}") for w in "ab"]
        meanvar_ready = [sem(f"meanvar_ready_{w}") for w in "ab"]
        var_ready = [sem(f"var_ready_{w}") for w in "ab"]
        rstd_ready = [sem(f"rstd_ready_{w}") for w in "ab"]
        shift_ready = [sem(f"shift_ready_{w}") for w in "ab"]
        ah_ready = sem("ah_ready")
        ynorm_ready, beta_added, ax_ready = sem("ynorm_ready"), sem("beta_added"), sem("ax_ready")
        ahead1_ready = sem("ahead1_ready")
        h_ready = sem("h_ready")
        high_ready, low_ready = sem("high_ready"), sem("low_ready")
        ahigh_ready, alow_ready = sem("ahigh_ready"), sem("alow_ready")
        hT_ready = sem("hT_ready")
        qk32_ready = sem("qk32_ready")
        part_high = sem("part_high")
        stacked = [sem(f"stacked{hd}") for hd in range(HEADS)]
        scores_ready, masked_ready, probs_ready = sem("scores_ready"), sem("masked_ready"), sem("probs_ready")
        turned = [sem(f"turned{i}") for i in range(2)]
        probT_ready = [sem(f"probT_ready{i}") for i in range(2)]
        summed, sum_kept = sem("summed"), sem("sum_kept")
        rwide_ready = sem("rwide_ready")
        att_ready = sem("att_ready")
        act_gate = sem("act_gate")
        dve_gate = sem("dve_gate")
        edgeT_ready, rank_ready, slots_summed, slots_known, table_ready = (
            sem("edgeT_ready"), sem("rank_ready"), sem("slots_summed"), sem("slots_known"), sem("table_ready"))
        limit_step, limited = sem("limit_step"), sem("limited")
        onehot_ready = sem("onehot_ready")
        extra_ready = sem("extra_ready")
        pooled = [sem(f"pooled{i}") for i in range(HALVES)]
        picked = [sem(f"picked{i}") for i in range(HALVES)]
        degwide_ready = sem("degwide_ready")
        pool_done = sem("pool_done")
        elu_dve, elu_act = sem("elu_dve"), sem("elu_act")
        stored = sem("stored")
        dve_small = sem("dve_small")

        with nc.Block() as block:
            LOADS = [(wq, A["wqT"]), (wk, A["wkT"]), (wv, A["wvT"]), (wo, A["woT"]), (wih, A["wihT"]),
                     (whh, A["whhT"]), (wmsgT, A["wmsgT"]), (wpool, A["wpool"]), (wroot, A["wroot"]),
                     (wrel, A["wrel"]), (cols, A["cols"]), (rows, A["rows"])]

            @block.sync
            def _(sp):
                for dst, src in LOADS:
                    sp.dma_start(dst[tuple([slice(None)] * len(dst.shape))], src).then_inc(const_loaded, 16)

            @block.gpsimd
            def _(pool):
                nc.gpsimd.memset(ident[:, :], 0.0).then_inc(ident_set, 1)
                nc.gpsimd.memset(ident16[:, :], 0.0).then_inc(ident_set, 1)
                nc.gpsimd.memset(upto[:, :], 0.0).then_inc(ident_set, 1)
                nc.gpsimd.memset(ones16[:, :], 1.0)
                nc.gpsimd.memset(minus_half[:, :], -0.5)
                nc.gpsimd.memset(ones_row[:, :], 1.0)
                for k in range(SLOTS + 1):
                    nc.gpsimd.memset(slotnum[:, k:k + 1], float(k + 1))
                pool.wait_ge(ident_set, 3)
                for m in (ident, ident16):
                    nc.gpsimd.affine_select(out=m[:, :], in_=m[:, :], compare_op=ALU.not_equal, fill=1.0,
                                            base=0, pattern=[[-1, P]], channel_multiplier=1).then_inc(ident_set, 1)
                nc.gpsimd.affine_select(out=upto[:, :], in_=upto[:, :], compare_op=ALU.is_gt, fill=1.0,
                                        base=0, pattern=[[-1, P]], channel_multiplier=1).then_inc(ident_set, 1)

            @block.tensor
            def _(pe):
                pe.wait_ge(const_loaded, 16 * len(LOADS))
                for layer in range(LAYERS):
                    nc.tensor.matmul(G[:, layer, 0:GATES * DIM], wmsgT[:, layer, :], wih[:, :],
                                     start=True, stop=True).then_inc(wgate_made, 1)

            @block.vector
            def _(dve):
                dve.wait_ge(const_loaded, 16 * len(LOADS))
                nc.vector.tensor_scalar(cols[:, BQ:BQ + 1], cols[:, BQ:BQ + 1], HEAD ** -0.5, None, op0=ALU.mult)
                nc.vector.tensor_tensor(half_b[:, 0:2], cols[:, BIH:BIH + 2], cols[:, BHH:BHH + 2],
                                        op=ALU.add).then_inc(dve_small, 1)
                dve.wait_ge(dve_small, 1)
                nc.vector.tensor_scalar(half_b[:, 0:2], half_b[:, 0:2], 0.5, None, op0=ALU.mult)
                nc.vector.tensor_scalar(half_b[:, 2:3], cols[:, BHH + 2:BHH + 3], 0.5, None, op0=ALU.mult)
                for layer in range(LAYERS):
                    dve.wait_ge(wgate_made, layer + 1)
                    nc.vector.tensor_copy(wgate[:, layer, :], G[:, layer, 0:GATES * DIM])

        nc.all_engine_barrier(sems_to_clear=range(sems[0].num, sems[-1].num + 1))

        def stages(block, ahead, graph):
            ORDER = [stage for stage in order_of() if (ahead, graph)[stage[0].startswith("b")] is not None]
            TURN = turn_table(ORDER)
            BANKS = {"a": AB, "b": G}

            def halves(j):
                return slice(j * HALF, (j + 1) * HALF), slice(j * PER_HALF, (j + 1) * PER_HALF)

            def in_tiles(bank):
                return bank.rearrange("p (t c) -> p t c", c=DIM)

            def place_of(name):
                w, i = TURN[name]
                bank = i % RINGS[w]
                return BANKS[w][:, bank, :], i // RINGS[w], filled[w][bank], drained[w][bank]

            def wait_filled(eng, name):
                bank, before, full, _ = place_of(name)
                eng.wait_ge(full, before + 1)
                return bank

            def wait_drained(eng, *names):
                for name in names:
                    _, before, _, empty = place_of(name)
                    eng.wait_ge(empty, before + 1)

            def is_drained(ins, name):
                ins.then_inc(place_of(name)[3], 1)

            def used_before(stage, w, bank):
                names = [n for s in ORDER[:ORDER.index(stage)] if s[0].startswith(w) for n in turns_of(s)]
                return sum(1 for i in range(len(names)) if i % RINGS[w] == bank)

            @block.sync
            def _(sp):
                if graph is not None:
                    sp.dma_start(edge1[:, :, :], ahead1[:, :, :]).then_inc(edge1_ready, 16)
                if ahead is not None:
                    sp.dma_start(ax[:, :, :], A["x"][bass.ds(ahead, 1), :, :]
                                 .rearrange("o (t p) c -> p (o t) c", p=P)).then_inc(x_loaded, 16)

                    def load_tile(t):
                        if t >= 2:
                            sp.wait_ge(ahead1_ready, t - 1)
                            sp.wait_ge(barred_ready, t - 1)
                        sp.dma_start(raw[:, t % 2, :], A["adj"][bass.ds(ahead, 1), t * P:(t + 1) * P, :]
                                     .rearrange("o p m -> p (o m)")).then_inc(raw_loaded[t % 2], 16)

                    load_tile(0)
                    load_tile(1)
                    wait_drained(sp, *(f"{w}_{j}" for w in "qk" for j in range(HALVES)))
                    for hd in range(HEADS):
                        for block_, (q_part, k_part) in enumerate(((0, 0), (1, 0), (0, 1), (1, 1))):
                            sp.dma_start(stack[HEAD * block_:HEAD * (block_ + 1), :, hd, :],
                                         all_parts[HEAD * hd:HEAD * (hd + 1), q_part:2 + k_part + 1:2 + k_part - q_part, :])\
                                .then_inc(stacked[hd], 16)
                    for t in range(2, TILES):
                        load_tile(t)
                if graph is not None:
                    wait_drained(sp, *(f"cnat{CONVS - 1}_{j}" for j in range(HALVES)))
                    sp.dma_start(out[bass.ds(graph, 1), :, :].rearrange("o (t p) c -> p (o t) c", p=P),
                                 h[:, :, :]).then_inc(stored, 16)
                    sp.wait_ge(stored, 16)

            @block.gpsimd
            def _(pool):
                def rstd_of(w, n):
                    pool.wait_ge(meanvar_ready[w], TILES * (n + 1))
                    nc.gpsimd.tensor_scalar(rstd[w][:, :], meanvar[w][:, :, 1], EPS, None,
                                            op0=ALU.add).then_inc(var_ready[w], 1)
                    pool.wait_ge(var_ready[w], n + 1)
                    nc.gpsimd.tensor_tensor(rstd[w][:, :], rstd[w][:, :], minus_half[:, :],
                                            op=ALU.pow).then_inc(rstd_ready[w], 1)

                def masks_ahead(t):
                    if graph is not None and t == 0:
                        pool.wait_ge(edge1_ready, 16)
                    pool.wait_ge(raw_loaded[t % 2], 16 * (t // 2 + 1))
                    nc.gpsimd.tensor_scalar(barred[:, t, :], raw[:, t % 2, :], 0.0, -BIG,
                                            op0=ALU.is_equal, op1=ALU.mult).then_inc(barred_ready, 1)
                    nc.gpsimd.tensor_scalar(ahead1[:, t, :], raw[:, t % 2, :], 1.0, F8_ONE,
                                            op0=ALU.is_equal, op1=ALU.mult).then_inc(ahead1_ready, 1)

                for stage in ORDER:
                    if stage == ("a_norm", 0):
                        masks_ahead(0)
                        masks_ahead(1)
                    elif stage[0] == "a_step" and stage[1] % HEADS == 0 and stage[1] // HEADS + 2 < TILES:
                        masks_ahead(stage[1] // HEADS + 2)
                    elif stage == ("a_q",):
                        pool.wait_ge(ah_ready, TILES)
                        nc.gpsimd.tensor_tensor(ax[:, :, :], ax[:, :, :],
                                                rows[:, BETA:BETA + 1, :].to_broadcast([P, TILES, DIM]),
                                                op=ALU.add).then_inc(beta_added, 1)
                    elif stage[0] == "b_stats":
                        rstd_of(1, stage[1])
                    elif stage[0] == "a_stats":
                        rstd_of(0, stage[1])
                    elif stage == ("a_limit",):
                        pool.wait_ge(outdeg_ready, TILES + 1)
                        nc.gpsimd.partition_all_reduce(maxdeg_all[:, :], maxdeg[:, :], P,
                                                       bass.bass_isa.ReduceOp.max).then_inc(maxdeg_ready, 1)
                    elif stage == ("b_rank", TILES - 1):
                        pool.wait_ge(slots_summed, 1)
                        nc.gpsimd.partition_all_reduce(slots_all[:, :], slots_f[:, :], P,
                                                       bass.bass_isa.ReduceOp.max).then_inc(slots_known, 1)

            @block.scalar
            def _(act):
                def affine(w, n, dst, src, func, done):
                    act.wait_ge(shift_ready[w], n + 1)
                    for t in range(TILES):
                        nc.scalar.activation(dst[:, t, :], src[:, t, :], func, scale=rstd[w][:, t:t + 1],
                                             bias=shift[w][:, t:t + 1]).then_inc(done, 1)

                def to_T(name, dst):
                    for j in range(HALVES):
                        bank = wait_filled(act, f"{name}_{j}")
                        is_drained(nc.scalar.activation(dst[:, halves(j)[0]], bank, ACT.Copy), f"{name}_{j}")

                def a_norm(n):
                    affine(0, 2 * n, ah, ax, ACT.Relu, ah_ready)
                    if n:
                        act.wait_ge(ah_ready, TILES * 2)
                        nc.scalar.activation(ahigh[:, :, :], ah[:, :, :], ACT.Copy).then_inc(ahigh_ready, 1)
                    to_T(f"ahT{n}", ahT)

                def a_part(i):
                    for j in range(HALVES):
                        act.wait_ge(qk32_ready, HALVES * i + j + 1)
                        nc.scalar.activation(parts[i][0][:, halves(j)[0]], qk32[i][:, halves(j)[0]],
                                             ACT.Copy).then_inc(part_high, 1)

                def a_step(s):
                    if s < STEPS:
                        act.wait_ge(masked_ready, s + 1)
                        if s >= 2:
                            act.wait_ge(turned[1], s - 1)
                        nc.scalar.activation(prob[:, s % 2, :], masked[:, s % 2, :], ACT.Exp, scale=-1.0,
                                             bias=negmax[:, s:s + 1], accum_out=rowsum[:, s:s + 1])\
                            .then_inc(probs_ready, 1)
                    if 1 <= s <= STEPS:
                        for j in range(2):
                            act.wait_ge(turned[j], s)
                            if s == RING - 1:
                                for hd in range(HEADS):
                                    act.wait_ge(stacked[hd], 16 * 4)
                            if s > RING:
                                act.wait_ge(summed, (s - 1 - RING) // HEADS + 1)
                            nc.scalar.activation(probT[:, (s - 1) % RING, j * PER_HALF:(j + 1) * PER_HALF, :],
                                                 in_tiles(PT[:, j, :]), ACT.Copy).then_inc(probT_ready[j], 1)

                def a_outdeg(t):
                    act.wait_ge(edge_ready, t + 1)
                    if t:
                        act.wait_ge(outdeg_ready, t)
                    nc.scalar.activation(ignored[:, :], edge[:, t, :], ACT.Copy,
                                         accum_out=outdeg[:, t:t + 1]).then_inc(outdeg_ready, 1)

                def b_norm(n):
                    affine(1, n, h, x, ACT.Relu, h_ready)
                    act.wait_ge(h_ready, TILES * (n + 1))
                    nc.scalar.activation(high[:, :, :], h[:, :, :], ACT.Copy).then_inc(high_ready, 1)
                    to_T(f"hT{n}", hT)

                def a_gather(layer, k):
                    for j in range(HALVES) if k else ():
                        name = f"u{layer}_{j}"
                        is_drained(nc.scalar.activation(auT[:, halves(j)[0]], wait_filled(act, name), ACT.Copy), name)

                def a_gates(layer, j):
                    g = 4 * j
                    for name, place, func, b_ in (("r", R, ACT.Tanh, 0), ("hn", X, ACT.Identity, 2),
                                                  ("z", Z, ACT.Tanh, 1)):
                        bank = wait_filled(act, f"{name}{layer}_{j}")
                        is_drained(nc.scalar.activation(gates[:, g + place, :], bank, func, scale=0.5,
                                                        bias=half_b[:, b_:b_ + 1]), f"{name}{layer}_{j}")
                    wait_drained(act, f"in{layer}_{j}")
                    nc.scalar.activation(gates[:, g + N, :], gates[:, g + X, :], ACT.Tanh,
                                         bias=cols[:, BIH + 2:BIH + 3]).then_inc(act_gate, 1)

                def high_of(dst, j, name, done):
                    nc.scalar.activation(dst[:, halves(j)[1], :], in_tiles(wait_filled(act, name)),
                                         ACT.Copy).then_inc(done, 1)

                def a_edgeT(t):
                    if graph is not None:
                        act.wait_ge(pool_done, 1)
                    bank = wait_filled(act, f"edgeT_{t}")
                    is_drained(nc.scalar.activation(edgeT[:, t, :], bank.bitcast(f16), ACT.Copy), f"edgeT_{t}")

                def b_degrec():
                    to_T("degrec", degrec)

                def b_conv(c, j):
                    act.wait_ge(elu_dve, (c * HALVES + j) * 2 + 1)
                    nc.scalar.activation(elu[:, 2 * j, :], elu[:, 2 * j, :], ACT.Exp).then_inc(elu_act, 1)

                for stage in ORDER:
                    name, args = stage[0], stage[1:]
                    if name == "a_norm":
                        a_norm(*args)
                    elif name in ("a_q", "a_k"):
                        a_part("qk".index(name[2]))
                    elif name == "a_step":
                        a_step(*args)
                    elif name == "a_ynorm":
                        affine(0, 1, ah, ah, ACT.Identity, ynorm_ready)
                    elif name == "a_gather":
                        a_gather(*args)
                    elif name == "a_gates":
                        a_gates(*args)
                    elif name == "a_outdeg":
                        a_outdeg(*args)
                    elif name == "a_natural" and args[0] < LAYERS - 1:
                        high_of(ahigh, args[1], f"nat{args[0]}_{args[1]}", ahigh_ready)
                    elif name == "a_edgeT":
                        a_edgeT(*args)
                    elif name == "b_norm":
                        b_norm(*args)
                    elif name == "b_degrec":
                        b_degrec()
                    elif name == "b_conv":
                        b_conv(*args)
                    elif name == "b_cnatural" and args[0] < CONVS - 1:
                        high_of(high, args[1], f"cnat{args[0]}_{args[1]}", high_ready)

            @block.tensor
            def _(pe):
                def fill(name):
                    bank, before, _, empty = place_of(name)
                    if before:
                        pe.wait_ge(empty, before)
                    return bank

                def is_full(ins, name):
                    ins.then_inc(place_of(name)[2], 1)

                def turn_half(name, j, src):
                    bank = fill(name)
                    for t in range(PER_HALF):
                        last = nc.tensor.transpose(bank[:, t * P:(t + 1) * P], src(j * PER_HALF + t), ident[:, :])
                    is_full(last, name)

                def in_T(src):
                    return lambda t: src[:, t * P:(t + 1) * P]

                def gather(name, k, parts, mask):
                    for j in range(HALVES):
                        bank = place_of(f"{name}_{j}")[0] if k else fill(f"{name}_{j}")
                        for t in range(k * PER_HALF, (k + 1) * PER_HALF):
                            for i, part in enumerate(parts):
                                last = nc.tensor.matmul(bank, part[:, t, :], mask[:, t, halves(j)[0]],
                                                        start=(t == 0 and i == 0), stop=(t == TILES - 1 and i == 1))
                        if k:
                            is_full(last, f"{name}_{j}")

                def a_norm(n):
                    for j in range(HALVES):
                        pe.wait_ge(ah_ready, TILES * n + PER_HALF * (j + 1))
                        turn_half(f"ahT{n}_{j}", j, lambda t: ah[:, t, :])

                def a_part(name, w):
                    for j in range(HALVES):
                        wait_drained(pe, f"ahT0_{j}")
                        bank = fill(f"{name}_{j}")
                        is_full(nc.tensor.matmul(bank, w[:, :], ahT[:, halves(j)[0]], start=True, stop=True),
                                f"{name}_{j}")

                def a_v():
                    for j in range(HALVES):
                        bank = fill(f"v_{j}")
                        for t in range(PER_HALF):
                            last = nc.tensor.matmul(bank[:, t * P:(t + 1) * P], in_T(ahT)(j * PER_HALF + t), wv[:, :],
                                                    start=True, stop=True)
                        is_full(last, f"v_{j}")

                def scores(s):
                    t, hd = s // HEADS, s % HEADS
                    if s < HEADS:
                        pe.wait_ge(stacked[hd], 16 * 4)
                    if s == 0:
                        for bank in (0, 1):
                            pe.wait_ge(drained["a"][bank], used_before(("a_step", 0), "a", bank))
                    else:
                        pe.wait_ge(masked_ready, s)
                    for j in range(HALVES):
                        last = nc.tensor.matmul(S[:, halves(j)[0]], qs[:, hd, t * P:(t + 1) * P],
                                                ks[:, hd, halves(j)[0]], start=True, stop=True)
                    last.then_inc(scores_ready, 1)

                def turn_probs(s):
                    pe.wait_ge(probs_ready, s + 1)
                    for j in range(2):
                        if s:
                            pe.wait_ge(probT_ready[j], s)
                        else:
                            pe.wait_ge(drained["a"][2 + j], used_before(("a_step", 0), "a", 2 + j))
                        for t in range(PER_HALF):
                            m = j * PER_HALF + t
                            last = nc.tensor.transpose(PT[:, j, t * P:(t + 1) * P],
                                                       prob[:, s % 2, m * P:(m + 1) * P], ident[:, :])
                        last.then_inc(turned[j], 1)

                def weigh(t, k):
                    if t == 0:
                        wait_drained(pe, "v_0", "v_1")
                    elif k == 0:
                        pe.wait_ge(sum_kept, t)
                    if k == 0:
                        for j in range(2):
                            pe.wait_ge(probT_ready[j], HEADS * (t + 1))
                    for m in range(k * PER_HALF, (k + 1) * PER_HALF):
                        for hd in range(HEADS):
                            last = nc.tensor.matmul(O[HEAD * hd:HEAD * (hd + 1), 0:P],
                                                    v[:, m, HEAD * hd:HEAD * (hd + 1)],
                                                    probT[:, (t * HEADS + hd) % RING, m, :],
                                                    start=(m == 0), stop=(m == TILES - 1))
                    if k:
                        last.then_inc(summed, 1)

                def a_step(s):
                    if s < STEPS:
                        scores(s)

                def a_turn(s):
                    if s > HEADS and s % HEADS == 2:
                        weigh(s // HEADS - 1, 1)
                    if 1 <= s <= STEPS:
                        turn_probs(s - 1)
                    if s > HEADS and s % HEADS == 1:
                        weigh(s // HEADS - 1, 0)

                def a_rinv():
                    pe.wait_ge(masked_ready, STEPS)
                    for j in range(2):
                        pe.wait_ge(probT_ready[j], STEPS)
                    pe.wait_ge(rwide_ready, 1)
                    for j in range(HALVES):
                        turn_half(f"rinvT_{j}", j, lambda t: rwide[:, t, :, :].rearrange("p a b -> p (a b)"))

                def a_y():
                    for j in range(HALVES):
                        pe.wait_ge(att_ready, j + 1)
                        bank = fill(f"y_{j}")
                        for t in range(PER_HALF):
                            last = nc.tensor.matmul(bank[:, t * P:(t + 1) * P], in_T(attU)(j * PER_HALF + t), wo[:, :],
                                                    start=True, stop=True)
                        is_full(last, f"y_{j}")

                def b_norm(n):
                    for j in range(HALVES):
                        pe.wait_ge(h_ready, TILES * n + PER_HALF * (j + 1))
                        turn_half(f"hT{n}_{j}", j, lambda t: h[:, t, :])

                def a_gather(layer, k):
                    if layer == 0:
                        pe.wait_ge(alow_ready, 1)
                        pe.wait_ge(edge_ready, TILES)
                    else:
                        wait_drained(pe, f"nat{layer - 1}_{k}")
                    gather(f"u{layer}", k, (ahigh, alow), edge)

                def a_gates(layer, j):
                    half = halves(j)[0]
                    wait_drained(pe, f"u{layer}_{j}")
                    if layer == 0:
                        wait_drained(pe, f"ahT1_{j}")

                    def gate(name, g, *sides):
                        bank = fill(f"{name}{layer}_{j}")
                        for k, (w, src) in enumerate(sides):
                            last = nc.tensor.matmul(bank, w[:, g * DIM:(g + 1) * DIM], src[:, half],
                                                    start=(k == 0), stop=(k == len(sides) - 1))
                        is_full(last, f"{name}{layer}_{j}")

                    wu = wgate[:, layer, :]
                    gate("r", 0, (wu, auT), (whh, ahT))
                    gate("hn", 2, (whh, ahT))
                    gate("in", 2, (wu, auT))
                    gate("z", 1, (wu, auT), (whh, ahT))

                def a_natural(layer, j):
                    pe.wait_ge(dve_gate, (layer * HALVES + j + 1) * 4)
                    turn_half(f"nat{layer}_{j}", j, in_T(ahT))

                def a_edgeT(t):
                    pe.wait_ge(limited, 1)
                    bank = fill(f"edgeT_{t}").bitcast(f16)
                    for n in range(TILES):
                        last = nc.tensor.transpose(bank[:, n * P:(n + 1) * P], edge[:, n, t * P:(t + 1) * P],
                                                   ident16[:, :])
                    is_full(last, f"edgeT_{t}")

                def b_rank(t):
                    for j in range(HALVES):
                        bank = fill(f"rank_{t}_{j}")
                        is_full(nc.tensor.matmul(bank, upto[:, :], edgeT[:, t, halves(j)[0]],
                                                 start=True, stop=True), f"rank_{t}_{j}")

                def pick(bank, t, half, hot):
                    nc.tensor.matmul(bank, high[:, t, :], hot[:, half], start=True, stop=False)
                    return nc.tensor.matmul(bank, low[:, t, :], hot[:, half], start=False, stop=True)

                def b_slot(i):
                    if i == 0:
                        pe.wait_ge(low_ready, 1)
                    pe.wait_ge(onehot_ready, i + 1)
                    for j in range(HALVES):
                        name = f"slot{i}_{j}"
                        is_full(pick(fill(name), i // FIXED, halves(j)[0], onehot[:, i % 2, :]), name)

                def b_extra():
                    for bank in range(HALVES):
                        pe.wait_ge(drained["b"][bank], used_before(("b_extra",), "b", bank))
                    pe.wait_ge(table_ready, 3)
                    more = pe.value_load(more_i[0:1, 0:1], min_val=0, max_val=(SLOTS - FIXED) * TILES)
                    with pe.If(more > 0):
                        for t in range(TILES):
                            extra = pe.value_load(extra_i[0:1, t:t + 1], min_val=0, max_val=SLOTS - FIXED)
                            first = pe.value_load(first_i[0:1, t:t + 1], min_val=0, max_val=(SLOTS - FIXED) * TILES)
                            with pe.If(extra > 0):
                                with pe.Fori(0, extra) as k:
                                    pe.wait_ge(extra_ready, first + (k + 1))
                                    for j in range(HALVES):
                                        pick(G[:, j, :], t, halves(j)[0], onehot[:, 0, :]).then_inc(picked[j], 1)
                    pe.wait_ge(pool_done, 1)

                def b_pool():
                    wait_drained(pe, "hT0_0", "hT0_1")
                    for j in range(HALVES):
                        bank = fill(f"pool_{j}")
                        for t in range(PER_HALF):
                            o, n = bank[:, t * P:(t + 1) * P], j * PER_HALF + t
                            nc.tensor.matmul(o, in_T(hT)(n), wpool[:, 0, :], start=True, stop=False)
                            last = nc.tensor.matmul(o, in_T(uT)(n), wpool[:, 1, :], start=False, stop=True)
                        is_full(last, f"pool_{j}")

                def b_degree():
                    pe.wait_ge(edge1_ready, 16)
                    bank = fill("degcol")
                    for t in range(TILES):
                        for n in range(TILES):
                            last = nc.tensor.matmul(bank[:, t:t + 1], edge1[:, n, t * P:(t + 1) * P].bitcast(f8),
                                                    ones16[:, 0:1], start=(n == 0), stop=(n == TILES - 1))
                    is_full(last, "degcol")

                def b_degrec():
                    pe.wait_ge(degwide_ready, 1)
                    for j in range(HALVES):
                        turn_half(f"degrec_{j}", j, lambda t: degwide[:, t, :])

                def b_cgather(c, k):
                    if c == 0:
                        pe.wait_ge(low_ready, 2)
                    else:
                        wait_drained(pe, f"cnat{c - 1}_{k}")
                    gather(f"cu{c}", k, (high, low), edge1[:, :, :].bitcast(f8))

                def b_conv(c, j):
                    if c == 0:
                        wait_drained(pe, f"hT1_{j}")
                    wait_drained(pe, f"cu{c}_{j}")
                    bank, half = fill(f"cy{c}_{j}"), halves(j)[0]
                    nc.tensor.matmul(bank, wroot[:, c, :], hT[:, half], start=True, stop=False)
                    is_full(nc.tensor.matmul(bank, wrel[:, c, :], uT[:, half], start=False, stop=True), f"cy{c}_{j}")

                def b_cnatural(c, j):
                    pe.wait_ge(elu_dve, (c * HALVES + j) * 2 + 2)
                    turn_half(f"cnat{c}_{j}", j, in_T(hT))

                for stage in ORDER:
                    name, args = stage[0], stage[1:]
                    if name == "a_norm":
                        a_norm(*args)
                    elif name == "a_q":
                        a_part("q", wq)
                    elif name == "a_k":
                        a_part("k", wk)
                    elif name == "a_v":
                        a_v()
                    elif name == "a_step":
                        a_step(*args)
                    elif name == "a_turn":
                        a_turn(*args)
                    elif name == "a_rinv":
                        a_rinv()
                    elif name == "a_y":
                        a_y()
                    elif name == "a_gather":
                        a_gather(*args)
                    elif name == "a_gates":
                        a_gates(*args)
                    elif name == "a_natural":
                        a_natural(*args)
                    elif name == "a_edgeT":
                        a_edgeT(*args)
                    elif name == "b_norm":
                        b_norm(*args)
                    elif name == "b_rank":
                        b_rank(*args)
                    elif name == "b_slot":
                        b_slot(*args)
                    elif name == "b_extra":
                        b_extra()
                    elif name == "b_pool":
                        b_pool()
                    elif name == "b_degree":
                        b_degree()
                    elif name == "b_degrec":
                        b_degrec()
                    elif name == "b_cgather":
                        b_cgather(*args)
                    elif name == "b_conv":
                        b_conv(*args)
                    elif name == "b_cnatural":
                        b_cnatural(*args)

            @block.vector
            def _(dve):
                small = [0]

                def link(ins):
                    small[0] += 1
                    ins.then_inc(dve_small, 1)
                    dve.wait_ge(dve_small, small[0])

                def mean_and_var(w, n, src):
                    for t in range(TILES):
                        nc.vector.bn_stats(stats[w][:, t, :], src[:, t, :]).then_inc(stats_ready[w], 1)
                    for t in range(TILES):
                        dve.wait_ge(stats_ready[w], TILES * n + t + 1)
                        nc.vector.bn_aggr(meanvar[w][:, t, :], stats[w][:, t, :]).then_inc(meanvar_ready[w], 1)

                def shift_of(w, n):
                    dve.wait_ge(rstd_ready[w], n + 1)
                    nc.vector.scalar_tensor_tensor(shift[w][:, :], meanvar[w][:, :, 0], -1.0, rstd[w][:, :],
                                                   op0=ALU.mult, op1=ALU.mult).then_inc(shift_ready[w], 1)

                def add_row(name, dst, row):
                    for j in range(HALVES):
                        bank = wait_filled(dve, f"{name}_{j}")
                        is_drained(nc.vector.tensor_tensor(
                            dst[:, halves(j)[1], :], in_tiles(bank),
                            rows[:, row:row + 1, :].to_broadcast([P, PER_HALF, DIM]), op=ALU.add), f"{name}_{j}")

                def a_stats(n):
                    if n == 0:
                        dve.wait_ge(x_loaded, 16)
                    elif n == 1:
                        wait_drained(dve, "y_0", "y_1")
                    mean_and_var(0, n, (ax, ah, ax)[n])

                def a_part(i):
                    for j in range(HALVES):
                        half, name = halves(j)[0], f"{'qk'[i]}_{j}"
                        nc.vector.tensor_scalar(qk32[i][:, half], wait_filled(dve, name), (HEAD ** -0.5, 1.0)[i],
                                                cols[:, BQ + i:BQ + i + 1], op0=ALU.mult,
                                                op1=ALU.add).then_inc(qk32_ready, 1)
                        dve.wait_ge(part_high, HALVES * i + j + 1)
                        is_drained(nc.vector.tensor_tensor(parts[i][1][:, half], qk32[i][:, half], parts[i][0][:, half],
                                                           op=ALU.subtract), name)

                def a_step(s):
                    if s < STEPS:
                        dve.wait_ge(scores_ready, s + 1)
                        dve.wait_ge(barred_ready, s // HEADS + 1)
                        if s >= 2:
                            dve.wait_ge(probs_ready, s - 1)
                        nc.vector.tensor_tensor_reduce(out=masked[:, s % 2, :], in0=S[:, :],
                                                       in1=barred[:, s // HEADS, :], scale=-1.0, scalar=3.0e38,
                                                       op0=ALU.add, op1=ALU.min,
                                                       accum_out=negmax[:, s:s + 1]).then_inc(masked_ready, 1)
                    if s > HEADS and s % HEADS == 3:
                        keep_sum(s // HEADS - 1)
                    if s >= HEADS and s % HEADS == 0:
                        t = s // HEADS - 1
                        nc.vector.tensor_scalar(edge[:, t, :], barred[:, t, :], 0.0, None,
                                                op0=ALU.is_equal).then_inc(edge_ready, 1)

                def keep_sum(t):
                    dve.wait_ge(summed, t + 1)
                    nc.vector.tensor_copy(attU[:, t * P:(t + 1) * P], O[:, 0:P]).then_inc(sum_kept, 1)

                def a_rinv():
                    keep_sum(TILES - 1)
                    dve.wait_ge(probs_ready, STEPS)
                    link(nc.vector.reciprocal(rinv[:, :], rowsum[:, :]))
                    nc.vector.tensor_copy(rwide[:, :, :, :].rearrange("p a b c -> p (a b) c"),
                                          rinv[:, :].unsqueeze(2).to_broadcast([P, STEPS, HEAD])).then_inc(rwide_ready, 1)
                    dve.wait_ge(sum_kept, TILES)
                    for j in range(HALVES):
                        half, name = halves(j)[0], f"rinvT_{j}"
                        nc.vector.tensor_tensor(attU[:, half], attU[:, half], wait_filled(dve, name),
                                                op=ALU.mult).then_inc(att_ready, 1)
                        dve.wait_ge(att_ready, j + 1)
                        dve.sem_inc(place_of(name)[3], 1)

                def a_gain():
                    dve.wait_ge(ynorm_ready, TILES)
                    link(nc.vector.tensor_tensor(ah[:, :, :], ah[:, :, :],
                                                 rows[:, GAMMA:GAMMA + 1, :].to_broadcast([P, TILES, DIM]),
                                                 op=ALU.mult))
                    dve.wait_ge(beta_added, 1)
                    link(nc.vector.tensor_tensor(ax[:, :, :], ax[:, :, :], ah[:, :, :], op=ALU.add))

                def a_end():
                    wait_drained(dve, *(f"nat{LAYERS - 1}_{j}" for j in range(HALVES)))
                    if graph is not None:
                        wait_drained(dve, *(f"cnat{CONVS - 1}_{j}" for j in range(HALVES)))
                    nc.vector.tensor_copy(x[:, :, :], ax[:, :, :]).then_inc(ax_ready, 1)

                def a_norm(n):
                    shift_of(0, 2 * n)
                    if n:
                        dve.wait_ge(ahigh_ready, 1)
                        nc.vector.tensor_tensor(alow[:, :, :], ah[:, :, :], ahigh[:, :, :],
                                                op=ALU.subtract).then_inc(alow_ready, 1)

                def b_norm(n):
                    shift_of(1, n)
                    dve.wait_ge(high_ready, n + 1)
                    nc.vector.tensor_tensor(low[:, :, :], h[:, :, :], high[:, :, :],
                                            op=ALU.subtract).then_inc(low_ready, 1)

                def a_gates(layer, j):
                    g, half, step = 4 * j, halves(j)[0], (layer * HALVES + j) * 4
                    wait_drained(dve, f"r{layer}_{j}", f"hn{layer}_{j}")
                    nc.vector.scalar_tensor_tensor(gates[:, g + X, :], gates[:, g + R, :], 1.0, gates[:, g + X, :],
                                                   op0=ALU.add, op1=ALU.mult).then_inc(dve_gate, 1)
                    dve.wait_ge(dve_gate, step + 1)
                    is_drained(nc.vector.tensor_tensor(gates[:, g + X, :], gates[:, g + X, :],
                                                       wait_filled(dve, f"in{layer}_{j}"), op=ALU.add),
                               f"in{layer}_{j}")
                    dve.wait_ge(act_gate, layer * HALVES + j + 1)
                    nc.vector.tensor_tensor(gates[:, g + R, :], ahT[:, half], gates[:, g + N, :],
                                            op=ALU.subtract).then_inc(dve_gate, 1)
                    dve.wait_ge(dve_gate, step + 2)
                    nc.vector.scalar_tensor_tensor(gates[:, g + R, :], gates[:, g + Z, :], 1.0, gates[:, g + R, :],
                                                   op0=ALU.add, op1=ALU.mult).then_inc(dve_gate, 1)
                    dve.wait_ge(dve_gate, step + 3)
                    nc.vector.scalar_tensor_tensor(ahT[:, half], gates[:, g + R, :], 0.5, gates[:, g + N, :],
                                                   op0=ALU.mult, op1=ALU.add).then_inc(dve_gate, 1)

                def low_of(dst, highs, j, name, high_is, high_count):
                    bank, tiles = in_tiles(wait_filled(dve, name)), halves(j)[1]
                    dve.wait_ge(high_is, high_count + j)
                    is_drained(nc.vector.tensor_tensor(dst[:, tiles, :], bank, highs[:, tiles, :],
                                                       op=ALU.subtract), name)

                def add_to(dst, src, j, name):
                    bank, tiles = in_tiles(wait_filled(dve, name)), halves(j)[1]
                    is_drained(nc.vector.tensor_tensor(dst[:, tiles, :], src[:, tiles, :], bank, op=ALU.add), name)

                def a_limit():
                    last = f"u{LAYERS - 1}"
                    wait_filled(dve, f"{last}_0")
                    wait_filled(dve, f"{last}_1")
                    dve.wait_ge(outdeg_ready, TILES)
                    nc.vector.tensor_reduce(maxdeg[:, :], outdeg[:, :], axis=AX.X, op=ALU.max).then_inc(outdeg_ready, 1)
                    dve.wait_ge(maxdeg_ready, 1)
                    link(nc.vector.tensor_copy(maxdeg_i[:, :], maxdeg_all[0:1, :]))
                    most = dve.value_load(maxdeg_i[0:1, 0:1], min_val=0, max_val=NODES)
                    with dve.If(most > SLOTS):
                        for t in range(TILES):
                            nc.vector.tensor_tensor_scan(count[:, :], ones_row[:, :], edge[:, t, :], 0.0, ALU.mult,
                                                         ALU.add).then_inc(limit_step, 1)
                            dve.wait_ge(limit_step, 2 * t + 1)
                            nc.vector.scalar_tensor_tensor(edge[:, t, :], count[:, :], float(SLOTS), edge[:, t, :],
                                                           op0=ALU.is_le, op1=ALU.mult).then_inc(limit_step, 1)
                            dve.wait_ge(limit_step, 2 * t + 2)
                    dve.sem_inc(limited, 1)

                def b_rank(t):
                    for j in range(HALVES):
                        here = edgeT[:, t, halves(j)[0]]
                        is_drained(nc.vector.tensor_tensor_reduce(
                            out=here, in0=wait_filled(dve, f"rank_{t}_{j}"), in1=here, scale=1.0, scalar=0.0,
                            op0=ALU.mult, op1=ALU.max, accum_out=maxrank[:, t, j:j + 1]), f"rank_{t}_{j}")
                    if t == TILES - 1:
                        wait_drained(dve, *(f"rank_{t}_{j}" for t in range(TILES) for j in range(HALVES)))
                        nc.vector.tensor_tensor(slots_f[:, :], maxrank[:, :, 0], maxrank[:, :, 1],
                                                op=ALU.max).then_inc(slots_summed, 1)

                def b_table():
                    dve.wait_ge(slots_known, 1)
                    link(nc.vector.tensor_scalar(slots_all[0:1, :], slots_all[0:1, :], -float(FIXED), 0.0,
                                                 op0=ALU.add, op1=ALU.max))
                    link(nc.vector.tensor_tensor_scan(first_f[:, :], ones_row[0:1, 0:TILES], slots_all[0:1, :], 0.0,
                                                      ALU.mult, ALU.add))
                    nc.vector.tensor_copy(extra_i[:, :], slots_all[0:1, :]).then_inc(table_ready, 1)
                    nc.vector.tensor_copy(more_i[:, :], first_f[:, TILES - 1:TILES]).then_inc(table_ready, 1)
                    nc.vector.tensor_tensor(first_i[:, :], first_f[:, :], slots_all[0:1, :],
                                            op=ALU.subtract).then_inc(table_ready, 1)
                    link(nc.vector.memset(uT[:, :], 0.0))
                    set_onehot(0)

                def set_onehot(i):
                    nc.vector.tensor_scalar(onehot[:, i % 2, :], edgeT[:, i // FIXED, :],
                                            slotnum[:, i % FIXED:i % FIXED + 1], None,
                                            op0=ALU.is_equal).then_inc(onehot_ready, 1)

                def b_slot(i):
                    if i + 1 < TILES * FIXED:
                        if i:
                            wait_filled(dve, f"slot{i - 1}_{HALVES - 1}")
                        set_onehot(i + 1)
                    for j in range(HALVES):
                        half, name = halves(j)[0], f"slot{i}_{j}"
                        if i:
                            wait_drained(dve, f"slot{i - 1}_{j}")
                        is_drained(nc.vector.tensor_tensor(uT[:, half], uT[:, half], wait_filled(dve, name),
                                                           op=ALU.max), name)

                def b_extra():
                    wait_drained(dve, *(f"slot{TILES * FIXED - 1}_{j}" for j in range(HALVES)))
                    dve.wait_ge(table_ready, 3)
                    for j in range(HALVES):
                        dve.sem_inc(pooled[j], 1)
                    more = dve.value_load(more_i[0:1, 0:1], min_val=0, max_val=(SLOTS - FIXED) * TILES)
                    with dve.If(more > 0):
                        for t in range(TILES):
                            extra = dve.value_load(extra_i[0:1, t:t + 1], min_val=0, max_val=SLOTS - FIXED)
                            first = dve.value_load(first_i[0:1, t:t + 1], min_val=0, max_val=(SLOTS - FIXED) * TILES)
                            with dve.If(extra > 0):
                                with dve.Fori(0, extra) as k:
                                    for j in range(HALVES):
                                        dve.wait_ge(pooled[j], first + (k + 1))
                                    nc.vector.tensor_scalar(onehot[:, 0, :], edgeT[:, t, :],
                                                            slotnum[:, bass.ds(k + FIXED, 1)], None,
                                                            op0=ALU.is_equal).then_inc(extra_ready, 1)
                                    for j in range(HALVES):
                                        half = halves(j)[0]
                                        dve.wait_ge(picked[j], first + (k + 1))
                                        nc.vector.tensor_tensor(uT[:, half], uT[:, half], G[:, j, :],
                                                                op=ALU.max).then_inc(pooled[j], 1)
                        for j in range(HALVES):
                            dve.wait_ge(pooled[j], more + 1)
                        dve.sem_inc(extra_ready, 1)
                    dve.sem_inc(pool_done, 1)

                def b_pool():
                    add_row("pool", h, BPOOL)
                    wait_drained(dve, "pool_0", "pool_1")
                    link(nc.vector.scalar_tensor_tensor(x[:, :, :], h[:, :, :], 0.0, x[:, :, :],
                                                        op0=ALU.max, op1=ALU.add))

                def b_degree():
                    is_drained(nc.vector.tensor_scalar(deg[:, :], wait_filled(dve, "degcol")[:, 0:TILES], 1.0, None,
                                                       op0=ALU.max), "degcol")
                    wait_drained(dve, "degcol")
                    link(nc.vector.reciprocal(deg[:, :], deg[:, :]))
                    nc.vector.tensor_copy(degwide[:, :, :],
                                          deg[:, :].unsqueeze(2).to_broadcast([P, TILES, P])).then_inc(degwide_ready, 1)

                def b_cgather(c, k):
                    for j in range(HALVES) if k else ():
                        bank, half = wait_filled(dve, f"cu{c}_{j}"), halves(j)[0]
                        wait_drained(dve, f"degrec_{j}")
                        is_drained(nc.vector.tensor_tensor(uT[:, half], bank, degrec[:, half], op=ALU.mult),
                                   f"cu{c}_{j}")

                def b_conv(c, j):
                    bias, half, name = cols[:, BCONV + c:BCONV + c + 1], halves(j)[0], f"cy{c}_{j}"
                    bank = wait_filled(dve, name)
                    nc.vector.tensor_scalar(elu[:, 2 * j, :], bank, bias, 0.0, op0=ALU.add,
                                            op1=ALU.min).then_inc(elu_dve, 1)
                    is_drained(nc.vector.tensor_scalar(elu[:, 2 * j + 1, :], bank, bias, 0.0, op0=ALU.add,
                                                       op1=ALU.max), name)
                    wait_drained(dve, name)
                    dve.wait_ge(elu_act, c * HALVES + j + 1)
                    nc.vector.scalar_tensor_tensor(hT[:, half], elu[:, 2 * j, :], -1.0, elu[:, 2 * j + 1, :],
                                                   op0=ALU.add, op1=ALU.add).then_inc(elu_dve, 1)

                for stage in ORDER:
                    name, args = stage[0], stage[1:]
                    if name == "a_stats":
                        a_stats(*args)
                    elif name == "a_norm":
                        a_norm(*args)
                    elif name in ("a_q", "a_k"):
                        a_part("qk".index(name[2]))
                    elif name == "a_v":
                        add_row("v", v, BV)
                    elif name == "a_step":
                        a_step(*args)
                    elif name == "a_rinv":
                        a_rinv()
                    elif name == "a_y":
                        add_row("y", ah, BO)
                    elif name == "a_ynorm":
                        shift_of(0, 1)
                    elif name == "a_gain":
                        a_gain()
                    elif name == "a_gates":
                        a_gates(*args)
                    elif name == "a_natural":
                        if args[0] < LAYERS - 1:
                            low_of(alow, ahigh, args[1], f"nat{args[0]}_{args[1]}", ahigh_ready, 2 + HALVES * args[0])
                        else:
                            add_to(ax, ax, args[1], f"nat{args[0]}_{args[1]}")
                    elif name == "a_limit":
                        a_limit()
                    elif name == "b_stats":
                        mean_and_var(1, args[0], x)
                    elif name == "b_norm":
                        b_norm(*args)
                    elif name == "b_rank":
                        b_rank(*args)
                    elif name == "b_table":
                        b_table()
                    elif name == "b_slot":
                        b_slot(*args)
                    elif name == "b_extra":
                        b_extra()
                    elif name == "b_pool":
                        b_pool()
                    elif name == "b_degree":
                        b_degree()
                    elif name == "b_cgather":
                        b_cgather(*args)
                    elif name == "b_conv":
                        b_conv(*args)
                    elif name == "b_cnatural":
                        if args[0] < CONVS - 1:
                            low_of(low, high, args[1], f"cnat{args[0]}_{args[1]}", high_ready, 3 + HALVES * args[0])
                        else:
                            add_to(h, x, args[1], f"cnat{args[0]}_{args[1]}")
                if ahead is not None:
                    a_end()

        def turn(ahead, graph):
            with nc.Block() as block:
                stages(block, ahead, graph)
            nc.all_engine_barrier(sems_to_clear=range(sems[0].num, sems[-1].num + 1))

        turn(0, None)
        with nc.Fori(0, BATCH - 1) as b:
            turn(b + 1, b)
        turn(None, BATCH - 1)


def kernel(**inputs):
    import numpy as np
    import concourse.bacc as bacc
    from concourse.bass_utils import run_bass_kernel_spmd

    a = {n: np.asarray(v) for n, v in inputs.items()}

    def column_blocks(v):
        return v.reshape(-1, 128).T

    layout = {
        "x": a["x"], "adj": a["adj"],
        "wqT": a["L0_gnn_Wq"].T, "wkT": a["L0_gnn_Wk"].T, "wvT": a["L0_gnn_Wv"].T, "woT": a["L0_gnn_Wo"].T,
        "wihT": a["L1_gnn_w_ih"].T, "whhT": a["L1_gnn_w_hh"].T,
        "wmsgT": a["L1_gnn_weight"].transpose(2, 0, 1),
        "wpool": a["L2_gnn_W"].reshape(2, 128, 128).transpose(1, 0, 2),
        "wroot": np.stack([a["L3_gnn_w_root1"], a["L3_gnn_w_root2"]], 1),
        "wrel": np.stack([a["L3_gnn_w_rel1"][1], a["L3_gnn_w_rel2"][1]], 1),
        "cols": np.concatenate([column_blocks(a[n]) for n in (
            "L0_gnn_bq", "L0_gnn_bk", "L1_gnn_b_ih", "L1_gnn_b_hh", "L3_gnn_b1", "L3_gnn_b2")], 1),
        "rows": np.broadcast_to(np.stack([a[n] for n in (
            "L0_gnn_bv", "L0_gnn_bo", "L0_gnn_gamma", "L0_gnn_beta", "L2_gnn_b")]), (128, 5, 128)),
    }
    nc = bacc.Bacc("TRN2", target_bir_lowering=False, num_devices=1)
    arrays, args = {}, {}
    for name, v in layout.items():
        v = np.ascontiguousarray(v)
        arrays[f"in_{name}_dram"] = v
        args[name] = nc.dram_tensor(f"in_{name}_dram", v.shape, mybir.dt.from_np(v.dtype), kind="ExternalInput").ap()
    out = nc.dram_tensor("out_0_dram", (BATCH, NODES, DIM), mybir.dt.float32, kind="ExternalOutput").ap()
    program(nc, args, out)
    r = run_bass_kernel_spmd(nc, [arrays], core_ids=[0])
    return r.results[0]["out_0_dram"]
```

```python
import concourse.bass as bass
from concourse import mybir
from contextlib import ExitStack

P = 128
BATCH, NODES, DIM = 8, 1024, 128
TILES = NODES // P
HEADS = 4
HEAD = DIM // HEADS
HALF = 512
HALVES = NODES // HALF
PER_HALF = HALF // P
LAYERS = 3
CONVS = 2
GATES = 3
STEPS = TILES * HEADS
RING = 5
SLOTS = 25
FIXED = 6
BIG = 2.0 ** 100
EPS = 1e-5
WSCALE = 64.0
F8_ONE = 0x38
FIRST_SLOTS, STEP_SLOTS = 1, 37
RINGS = {"a": 4, "b": 3}


def order_of():
    order = [("b_stats", 0), ("b_counts",), ("a_turnh", 0), ("b_table",), ("a_q",), ("a_k",), ("a_v",),
             ("b_rank", 0), ("b_affine", 0, 0), ("b_degree",), ("b_first",), ("b_affine", 0, 1), ("b_turnh", 0),
             ("b_rank", 1), ("a_barred", 0), ("b_degrec",), ("b_slot", 0)]
    taken = FIRST_SLOTS
    for step in range(STEPS + 3):
        upto = FIRST_SLOTS + (step + 1) * (STEP_SLOTS - FIRST_SLOTS) // (STEPS + 3)
        if step < TILES - 2:
            order.append(("b_rank", step + 2))
        order += [("a_step", step)] + [("b_slot", i) for i in range(taken, upto)] + [("a_turn", step)]
        taken = upto
        if step % HEADS == 0 and step // HEADS < TILES:
            order.append(("a_ahead1", step // HEADS))
        if step % HEADS == 1 and step // HEADS + 1 < TILES:
            order.append(("a_barred", step // HEADS + 1))
        if step == 2:
            order.append(("a_beta",))
    order += [("a_rinv",), ("a_edge", 0), ("b_slot", 37), ("a_edge", 1), ("a_edge", 2), ("a_edge", 3),
              ("b_slot", 38), ("a_y",), ("a_edge", 4), ("a_stats", 0), ("a_edge", 5), ("a_edge", 6), ("a_edge", 7),
              ("a_maxdeg",), ("b_slot", 39), ("b_slot", 40), ("a_ynorm",), ("b_slot", 41), ("b_slot", 42),
              ("a_gain",), ("a_stats", 1), ("b_slot", 43), ("b_slot", 44), ("a_affine", 0), ("b_slot", 45),
              ("a_affine", 1), ("b_slot", 46), ("a_turnh", 1), ("b_slot", 47)]
    order += [("a_gather", 0, 0), ("b_extra",), ("a_gather", 0, 1), ("a_gates", 0, 0), ("b_pool",),
              ("a_natural", 0, 0), ("a_gates", 0, 1), ("b_stats", 1), ("a_gather", 1, 0), ("a_natural", 0, 1),
              ("b_affine", 1, 0), ("a_gather", 1, 1), ("a_gates", 1, 0), ("b_affine", 1, 1), ("b_cgather", 0, 0),
              ("a_natural", 1, 0), ("b_cgather", 0, 1), ("b_turnh", 1), ("a_gates", 1, 1), ("c_stats",),
              ("a_gather", 2, 0), ("b_conv", 0, 0), ("a_natural", 1, 1), ("b_conv", 0, 1), ("a_gather", 2, 1),
              ("b_cnatural", 0, 0), ("b_cnatural", 0, 1), ("a_limit",), ("a_gates", 2, 0), ("b_cgather", 1, 0),
              ("c_affine", 0), ("c_affine", 1), ("a_edgeT", 0), ("b_cgather", 1, 1), ("a_edgeT", 1),
              ("a_natural", 2, 0), ("a_edgeT", 2), ("b_conv", 1, 0), ("b_conv", 1, 1), ("a_gates", 2, 1),
              ("a_edgeT", 3), ("a_edgeT", 4), ("b_cnatural", 1, 0), ("b_cnatural", 1, 1), ("a_edgeT", 5),
              ("a_edgeT", 6), ("a_natural", 2, 1), ("a_edgeT", 7)]
    return order


def turns_of(stage):
    name, rest = stage[0], "_".join(map(str, stage[1:]))
    both = {"a_turnh": "ahT" + rest, "a_q": "q", "a_k": "k", "a_v": "v", "a_rinv": "rinvT", "a_y": "y",
            "b_turnh": "hT" + rest, "b_pool": "pool", "b_degrec": "degrec"}
    if name in both:
        return [f"{both[name]}_{j}" for j in range(HALVES)]
    if name in ("a_gather", "b_cgather"):
        u = "u" if name == "a_gather" else "cu"
        return [f"{u}{stage[1]}_{j}" for j in range(HALVES)] if stage[2] == 0 else []
    if name in ("a_natural", "b_cnatural"):
        return [("nat" if name == "a_natural" else "cnat") + rest]
    if name == "a_gates":
        return [g + rest for g in ("r", "hn", "in", "z")]
    if name == "a_edgeT":
        return ["edgeT_" + rest]
    if name == "b_counts":
        return ["counts"]
    if name == "b_degree":
        return ["degcol"]
    if name == "b_slot":
        return [f"slot{rest}_{j}" for j in range(HALVES)]
    if name == "b_rank":
        return [f"rank_{rest}_{j}" for j in range(HALVES)]
    if name == "b_conv":
        return ["cy" + rest]
    return []


def turn_table(order):
    table = {}
    for stream in RINGS:
        names = [n for stage in order if stage[0].startswith(stream) for n in turns_of(stage)]
        table.update((name, (stream, i)) for i, name in enumerate(names))
    return table


def program(nc, A, out):
    f32, f16, bf16 = mybir.dt.float32, mybir.dt.float16, mybir.dt.bfloat16
    i32, f8 = mybir.dt.int32, mybir.dt.float8e4
    u8 = mybir.dt.uint8
    ALU = mybir.AluOpType
    ACT = mybir.ActivationFunctionType
    AX = mybir.AxisListType

    ctx = ExitStack()
    with ctx:
        def sb(name, shape, dt):
            return ctx.enter_context(nc.sbuf_tensor(name, shape, dt))

        def sem(name):
            s = ctx.enter_context(nc.semaphore(name))
            sems.append(s)
            return s

        sems = []

        ident = sb("ident", [P, P], f32)
        ident16 = sb("ident16", [P, P], f16)
        before = sb("before", [P, P], f16)
        ones16 = sb("ones16", [P, P], f16)
        wq, wk, wv, wo = (sb(n, [P, DIM], f32) for n in ("wq", "wk", "wv", "wo"))
        wih = sb("wih", [P, GATES * DIM], f32)
        whh = sb("whh", [P, GATES * DIM], f32)
        wmsgT = sb("wmsgT", [P, LAYERS, DIM], f32)
        wgate = sb("wgate", [P, 2, LAYERS, GATES * DIM], f16)
        whh2 = sb("whh2", [P, 2, GATES * DIM], f16)
        wpool = sb("wpool", [P, 2, DIM], f32)
        wroot = sb("wroot", [P, CONVS, DIM], f32)
        wrel = sb("wrel", [P, CONVS, DIM], f32)
        cols = sb("cols", [P, 10], f32)
        BQ, BK, BIH, BHH, BCONV = 0, 1, 2, 5, 8
        rows = sb("rows", [P, 5, DIM], f32)
        BV, BO, GAMMA, BETA, BPOOL = range(5)
        half_b = sb("half_b", [P, 3], f32)
        minus_half = sb("minus_half", [P, TILES], f32)
        one, minus_one, f8_one = (sb(n, [P, 1], f32) for n in ("one", "minus_one", "f8_one"))
        ones_row = sb("ones_row", [P, NODES], f16)
        slotnum = sb("slotnum", [P, SLOTS + 1], f32)

        raw = sb("raw", [P, 2, NODES], i32)
        edge = sb("edge", [P, TILES, NODES], f16)
        barred = edge[:, :, :].rearrange("p t n -> p (t n)").bitcast(bf16)\
            .rearrange("p (t n) -> p t n", t=TILES)
        edge1 = sb("edge1", [P, TILES, NODES], u8)
        ahead1 = sb("ahead1", [P, TILES, NODES], u8)
        x = sb("x", [P, TILES, DIM], f32)
        ax = sb("ax", [P, TILES, DIM], f32)
        ah = sb("ah", [P, TILES, DIM], f32)
        ahT = sb("ahT", [P, NODES], f32)
        h = sb("h", [P, TILES, DIM], f32)
        hT = sb("hT", [P, NODES], f32)
        high = sb("high", [P, TILES, DIM], f16)
        low = sb("low", [P, TILES, DIM], f16)
        ahigh = sb("ahigh", [P, TILES, DIM], f16)
        alow = sb("alow", [P, TILES, DIM], f16)
        stats = [sb(f"stats_{w}", [P, TILES, 6], f32) for w in "abc"]
        meanvar = [sb(f"meanvar_{w}", [P, TILES, 2], f32) for w in "abc"]
        rstd = [sb(f"rstd_{w}", [P, TILES], f32) for w in "abc"]
        shift = [sb(f"shift_{w}", [P, TILES], f32) for w in "abc"]
        distance = sb("distance", [P, NODES], bf16)
        stack = sb("stack", [P, 2, HEADS, NODES], f16)
        qs, ks = stack[:, 0, :, :], stack[:, 1, :, :]
        v = sb("v", [P, TILES, DIM], f32)
        masked = sb("masked", [P, 2, NODES], f32)
        prob = sb("prob", [P, 2, NODES], f32)
        probT = sb("probT", [P, RING, TILES, P], f32)
        all_parts = probT[:, RING - 2:RING, :, :].rearrange("p a t n -> p (a t n)").bitcast(f16)\
            .rearrange("p (a n) -> p a n", a=4)
        parts = [[all_parts[:, 2 * i + a, :] for a in range(2)] for i in range(2)]
        negmax = sb("negmax", [P, STEPS], f32)
        rowsum = sb("rowsum", [P, STEPS], f32)
        attU = sb("attU", [P, NODES], f32)
        rinv = sb("rinv", [P, STEPS], f32)
        rwide = sb("rwide", [P, TILES, HEADS, HEAD], f32)
        qk32 = [attU, rwide[:, :, :, :].rearrange("p a b c -> p (a b c)")]
        uT = sb("uT", [P, NODES], f32)
        auT = attU[:, :].bitcast(f16).rearrange("p (k n) -> p k n", k=2)
        ahT2 = sb("ahT2", [P, 2, NODES], f16)
        gates = stack[:, :, :, :].rearrange("p a b c -> p (a b c)").bitcast(f32)\
            .rearrange("p (g n) -> p g n", g=8)
        R, X, Z, N = range(4)
        elu = sb("elu", [P, 4, HALF], f32)
        edgeT = sb("edgeT", [P, TILES, NODES], f16)
        onehot = sb("onehot", [P, 2, NODES], f16)
        slots_f = sb("slots_f", [P, TILES], f32)
        slots_all = sb("slots_all", [P, TILES], f32)
        first_f = sb("first_f", [1, TILES], f32)
        extra_i = sb("extra_i", [1, TILES], i32)
        more_i = sb("more_i", [1, 1], i32)
        first_i = sb("first_i", [1, TILES], i32)
        outdeg = sb("outdeg", [P, TILES], f32)
        maxdeg = sb("maxdeg", [P, 1], f32)
        maxdeg_all = sb("maxdeg_all", [P, 1], f32)
        maxdeg_i = sb("maxdeg_i", [1, 1], i32)
        count = distance[:, :].bitcast(f16)
        deg = sb("deg", [P, TILES], f32)
        degwide = elu[:, 0:2, :].rearrange("p a b -> p (a b)").rearrange("p (t c) -> p t c", t=TILES)
        degrec = sb("degrec", [P, NODES], f32)

        AB = ctx.enter_context(nc.psum_tensor("AB", [P, RINGS["a"], HALF], f32))
        S = AB[:, 0:2, :].rearrange("p a b -> p (a b)")
        PT = AB[:, 2:4, :]
        O = ctx.enter_context(nc.psum_tensor("O", [P, HALF], f32))
        G = ctx.enter_context(nc.psum_tensor("G", [P, RINGS["b"], HALF], f32))

        const_loaded = sem("const_loaded")
        ident_set = sem("ident_set")
        wgate_made = sem("wgate_made")
        x_loaded = sem("x_loaded")
        next_loaded, next_ready = sem("next_loaded"), sem("next_ready")
        raw_loaded = [sem(f"raw_loaded{i}") for i in range(2)]
        edge_ready, edge1_ready, barred_ready = sem("edge_ready"), sem("edge1_ready"), sem("barred_ready")
        distance_ready = sem("distance_ready")
        maxdeg_ready = sem("maxdeg_ready")
        filled = {w: [sem(f"filled_{w}{i}") for i in range(n)] for w, n in RINGS.items()}
        drained = {w: [sem(f"drained_{w}{i}") for i in range(n)] for w, n in RINGS.items()}
        stats_ready = [sem(f"stats_ready_{w}") for w in "abc"]
        meanvar_ready = [sem(f"meanvar_ready_{w}") for w in "abc"]
        var_ready = [sem(f"var_ready_{w}") for w in "abc"]
        rstd_ready = [sem(f"rstd_ready_{w}") for w in "abc"]
        shift_ready = [sem(f"shift_ready_{w}") for w in "abc"]
        ah_ready = sem("ah_ready")
        ynorm_ready, beta_added, ax_ready = sem("ynorm_ready"), sem("beta_added"), sem("ax_ready")
        ahead1_ready = sem("ahead1_ready")
        h_ready = sem("h_ready")
        high_ready, low_ready = sem("high_ready"), sem("low_ready")
        ahigh_ready, alow_ready = sem("ahigh_ready"), sem("alow_ready")
        part_high, part_low = sem("part_high"), sem("part_low")
        stacked = [sem(f"stacked{hd}") for hd in range(HEADS)]
        scores_ready, masked_ready, probs_ready = sem("scores_ready"), sem("masked_ready"), sem("probs_ready")
        turned = [sem(f"turned{i}") for i in range(2)]
        probT_ready = [sem(f"probT_ready{i}") for i in range(2)]
        summed, sum_kept = sem("summed"), sem("sum_kept")
        rwide_ready = sem("rwide_ready")
        att_ready = sem("att_ready")
        act_gate = sem("act_gate")
        sum_high, state_high, state_low = sem("sum_high"), sem("state_high"), sem("state_low")
        dve_gate = sem("dve_gate")
        slots_known, table_ready = sem("slots_known"), sem("table_ready")
        limit_step, limited = sem("limit_step"), sem("limited")
        onehot_ready = sem("onehot_ready")
        extra_ready = sem("extra_ready")
        pooled = [sem(f"pooled{i}") for i in range(HALVES)]
        picked = [sem(f"picked{i}") for i in range(HALVES)]
        degwide_ready = sem("degwide_ready")
        pool_done = sem("pool_done")
        elu_dve, elu_act = sem("elu_dve"), sem("elu_act")
        stored = sem("stored")
        dve_small = sem("dve_small")

        with nc.Block() as block:
            LOADS = [(wq, A["wqT"]), (wk, A["wkT"]), (wv, A["wvT"]), (wo, A["woT"]), (wih, A["wihT"]),
                     (whh, A["whhT"]), (wmsgT, A["wmsgT"]), (wpool, A["wpool"]), (wroot, A["wroot"]),
                     (wrel, A["wrel"]), (cols, A["cols"]), (rows, A["rows"])]

            @block.sync
            def _(sp):
                for dst, src in LOADS:
                    sp.dma_start(dst[tuple([slice(None)] * len(dst.shape))], src).then_inc(const_loaded, 16)

            @block.gpsimd
            def _(pool):
                nc.gpsimd.memset(ident[:, :], 0.0).then_inc(ident_set, 1)
                nc.gpsimd.memset(ident16[:, :], 0.0).then_inc(ident_set, 1)
                nc.gpsimd.memset(before[:, :], 0.0).then_inc(ident_set, 1)
                nc.gpsimd.memset(ones16[:, :], 1.0)
                nc.gpsimd.memset(minus_half[:, :], -0.5)
                nc.gpsimd.memset(one[:, :], 1.0)
                nc.gpsimd.memset(minus_one[:, :], -1.0)
                nc.gpsimd.memset(f8_one[:, :], float(F8_ONE))
                nc.gpsimd.memset(ones_row[:, :], 1.0)
                for k in range(SLOTS + 1):
                    nc.gpsimd.memset(slotnum[:, k:k + 1], float(2 * k + 1))
                pool.wait_ge(ident_set, 3)
                for m in (ident, ident16):
                    nc.gpsimd.affine_select(out=m[:, :], in_=m[:, :], compare_op=ALU.not_equal, fill=1.0,
                                            base=0, pattern=[[-1, P]], channel_multiplier=1).then_inc(ident_set, 1)
                nc.gpsimd.affine_select(out=before[:, :], in_=before[:, :], compare_op=ALU.is_ge, fill=2.0,
                                        base=0, pattern=[[-1, P]], channel_multiplier=1).then_inc(ident_set, 1)
                pool.wait_ge(ident_set, 6)
                nc.gpsimd.affine_select(out=before[:, :], in_=before[:, :], compare_op=ALU.not_equal, fill=1.0,
                                        base=0, pattern=[[-1, P]], channel_multiplier=1).then_inc(ident_set, 1)

            @block.tensor
            def _(pe):
                pe.wait_ge(const_loaded, 16 * len(LOADS))
                for layer in range(LAYERS):
                    nc.tensor.matmul(G[:, layer, 0:GATES * DIM], wmsgT[:, layer, :], wih[:, :],
                                     start=True, stop=True).then_inc(wgate_made, 1)

            @block.vector
            def _(dve):
                dve.wait_ge(const_loaded, 16 * len(LOADS))
                nc.vector.tensor_scalar(cols[:, BQ:BQ + 1], cols[:, BQ:BQ + 1], HEAD ** -0.5, None, op0=ALU.mult)
                small = [0]

                def link(ins):
                    small[0] += 1
                    ins.then_inc(dve_small, 1)
                    dve.wait_ge(dve_small, small[0])

                def in_parts(w, w_high, w_low):
                    link(nc.vector.tensor_scalar(w_high, w, WSCALE, None, op0=ALU.mult))
                    nc.vector.scalar_tensor_tensor(w_low, w, WSCALE, w_high, op0=ALU.mult, op1=ALU.subtract)

                link(nc.vector.tensor_tensor(half_b[:, 0:2], cols[:, BIH:BIH + 2], cols[:, BHH:BHH + 2], op=ALU.add))
                nc.vector.tensor_scalar(half_b[:, 0:2], half_b[:, 0:2], 0.5, None, op0=ALU.mult)
                nc.vector.tensor_scalar(half_b[:, 2:3], cols[:, BHH + 2:BHH + 3], 0.5, None, op0=ALU.mult)
                for layer in range(LAYERS):
                    dve.wait_ge(wgate_made, layer + 1)
                    in_parts(G[:, layer, 0:GATES * DIM], wgate[:, 0, layer, :], wgate[:, 1, layer, :])
                in_parts(whh[:, :], whh2[:, 0, :], whh2[:, 1, :])

        nc.all_engine_barrier(sems_to_clear=range(sems[0].num, sems[-1].num + 1))

        def stages(block, following, ahead, graph):
            GRAPH_OF = {"a": ahead, "b": graph, "c": following}
            ORDER = [stage for stage in order_of() if GRAPH_OF[stage[0][0]] is not None]
            TURN = turn_table(ORDER)
            BANKS = {"a": AB, "b": G}

            def halves(j):
                return slice(j * HALF, (j + 1) * HALF), slice(j * PER_HALF, (j + 1) * PER_HALF)

            def in_tiles(bank):
                return bank.rearrange("p (t c) -> p t c", c=DIM)

            def place_of(name):
                w, i = TURN[name]
                bank = i % RINGS[w]
                return BANKS[w][:, bank, :], i // RINGS[w], filled[w][bank], drained[w][bank]

            def wait_filled(eng, name):
                bank, before, full, _ = place_of(name)
                eng.wait_ge(full, before + 1)
                return bank

            def wait_drained(eng, *names):
                for name in names:
                    _, before, _, empty = place_of(name)
                    eng.wait_ge(empty, before + 1)

            def is_drained(ins, name):
                ins.then_inc(place_of(name)[3], 1)

            def used_before(stage, w, bank):
                names = [n for s in ORDER[:ORDER.index(stage)] if s[0].startswith(w) for n in turns_of(s)]
                return sum(1 for i in range(len(names)) if i % RINGS[w] == bank)

            @block.sync
            def _(sp):
                if ahead is not None:
                    def load_tile(t):
                        if t >= 2:
                            sp.wait_ge(ahead1_ready, t - 1)
                            sp.wait_ge(barred_ready, t - 1)
                        sp.dma_start(raw[:, t % 2, :], A["adj"][bass.ds(ahead, 1), t * P:(t + 1) * P, :]
                                     .rearrange("o p m -> p (o m)")).then_inc(raw_loaded[t % 2], 16)

                    load_tile(0)
                if graph is not None:
                    sp.dma_start(edge1[:, :, :], ahead1[:, :, :]).then_inc(edge1_ready, 16)
                if ahead is not None:
                    load_tile(1)
                    sp.dma_start(ax[:, :, :], A["x"][bass.ds(ahead, 1), :, :]
                                 .rearrange("o (t p) c -> p (o t) c", p=P)).then_inc(x_loaded, 16)
                    sp.wait_ge(part_low, 2 * HALVES)
                    for hd in range(HEADS):
                        for block_, (q_part, k_part) in enumerate(((0, 0), (1, 0), (0, 1), (1, 1))):
                            both = slice(q_part, 2 + k_part + 1, 2 + k_part - q_part)
                            sp.dma_start(stack[HEAD * block_:HEAD * (block_ + 1), :, hd, :],
                                         all_parts[HEAD * hd:HEAD * (hd + 1), both, :]).then_inc(stacked[hd], 16)
                    for t in range(2, TILES):
                        load_tile(t)
                if following is not None:
                    if ahead is not None:
                        wait_filled(sp, f"ahT1_{HALVES - 1}")
                        sp.wait_ge(alow_ready, HALVES)
                    sp.dma_start(ah[:, :, :], A["x"][bass.ds(following, 1), :, :]
                                 .rearrange("o (t p) c -> p (o t) c", p=P)).then_inc(next_loaded, 16)
                if graph is not None:
                    wait_drained(sp, *(f"cnat{CONVS - 1}_{j}" for j in range(HALVES)))
                    sp.dma_start(out[bass.ds(graph, 1), :, :].rearrange("o (t p) c -> p (o t) c", p=P),
                                 h[:, :, :]).then_inc(stored, 16)
                    sp.wait_ge(stored, 16)

            @block.gpsimd
            def _(pool):
                def rstd_of(w, n):
                    pool.wait_ge(meanvar_ready[w], TILES * (n + 1))
                    nc.gpsimd.tensor_scalar(rstd[w][:, :], meanvar[w][:, :, 1], EPS, None,
                                            op0=ALU.add).then_inc(var_ready[w], 1)
                    pool.wait_ge(var_ready[w], n + 1)
                    nc.gpsimd.tensor_tensor(rstd[w][:, :], rstd[w][:, :], minus_half[:, :],
                                            op=ALU.pow).then_inc(rstd_ready[w], 1)

                for stage in ORDER:
                    if stage == ("a_beta",):
                        pool.wait_ge(x_loaded, 16)
                        nc.gpsimd.tensor_tensor(ax[:, :, :], ax[:, :, :],
                                                rows[:, BETA:BETA + 1, :].to_broadcast([P, TILES, DIM]),
                                                op=ALU.add).then_inc(beta_added, 1)
                    elif stage[0] == "b_stats":
                        rstd_of(1, stage[1])
                    elif stage[0] == "a_stats":
                        rstd_of(0, stage[1])
                    elif stage[0] == "c_stats":
                        rstd_of(2, 0)
                    elif stage == ("a_maxdeg",):
                        pool.wait_ge(edge_ready, TILES + 1)
                        nc.gpsimd.partition_all_reduce(maxdeg_all[:, :], maxdeg[:, :], P,
                                                       bass.bass_isa.ReduceOp.max).then_inc(maxdeg_ready, 1)
                    elif stage == ("b_counts",):
                        wait_drained(pool, "counts")
                        nc.gpsimd.partition_all_reduce(slots_all[:, :], slots_f[:, :], P,
                                                       bass.bass_isa.ReduceOp.max).then_inc(slots_known, 1)

            @block.scalar
            def _(act):
                def affine(w, n, j, dst, src, func, done):
                    act.wait_ge(shift_ready[w], n + 1)
                    for t in range(j * PER_HALF, (j + 1) * PER_HALF):
                        nc.scalar.activation(dst[:, t, :], src[:, t, :], func, scale=rstd[w][:, t:t + 1],
                                             bias=shift[w][:, t:t + 1]).then_inc(done, 1)

                def high_part(dst, src, j, src_ready, count, done):
                    act.wait_ge(src_ready, count)
                    nc.scalar.activation(dst[:, halves(j)[1], :], src[:, halves(j)[1], :], ACT.Copy).then_inc(done, 1)

                def to_T(name, dst):
                    for j in range(HALVES):
                        bank = wait_filled(act, f"{name}_{j}")
                        is_drained(nc.scalar.activation(dst[:, halves(j)[0]], bank, ACT.Copy), f"{name}_{j}")

                def a_affine(j):
                    affine(0, 1, j, ah, ax, ACT.Relu, ah_ready)
                    high_part(ahigh, ah, j, ah_ready, PER_HALF * (j + 1), ahigh_ready)

                def a_part(i):
                    for j in range(HALVES):
                        name = f"{'qk'[i]}_{j}"
                        is_drained(nc.scalar.activation(qk32[i][:, halves(j)[0]], wait_filled(act, name), ACT.Identity,
                                                        scale=(HEAD ** -0.5, 1.0)[i], bias=cols[:, BQ + i:BQ + i + 1]),
                                   name)
                        wait_drained(act, name)
                        nc.scalar.activation(parts[i][0][:, halves(j)[0]], qk32[i][:, halves(j)[0]],
                                             ACT.Copy).then_inc(part_high, 1)

                def a_step(s):
                    if s < STEPS:
                        act.wait_ge(masked_ready, s + 1)
                        if s >= 2:
                            act.wait_ge(turned[1], s - 1)
                        nc.scalar.activation(prob[:, s % 2, :], masked[:, s % 2, :], ACT.Exp, scale=-1.0,
                                             bias=negmax[:, s:s + 1], accum_out=rowsum[:, s:s + 1])\
                            .then_inc(probs_ready, 1)
                    if 1 <= s <= STEPS:
                        for j in range(2):
                            act.wait_ge(turned[j], s)
                            if s == RING - 1:
                                for hd in range(HEADS):
                                    act.wait_ge(stacked[hd], 16 * 4)
                            if s > RING:
                                act.wait_ge(summed, (s - 1 - RING) // HEADS + 1)
                            nc.scalar.activation(probT[:, (s - 1) % RING, j * PER_HALF:(j + 1) * PER_HALF, :],
                                                 in_tiles(PT[:, j, :]), ACT.Copy).then_inc(probT_ready[j], 1)

                def a_ahead1(t):
                    if graph is not None:
                        act.wait_ge(edge1_ready, 16)
                    if t:
                        act.wait_ge(ahead1_ready, t)
                    act.wait_ge(raw_loaded[t % 2], 16 * (t // 2 + 1))
                    nc.scalar.activation(distance[:, :], raw[:, t % 2, :], ACT.Abs,
                                         bias=minus_one[:, :]).then_inc(distance_ready, 1)
                    act.wait_ge(distance_ready, t + 1)
                    nc.scalar.activation(ahead1[:, t, :], distance[:, :], ACT.Relu, scale=-float(F8_ONE),
                                         bias=f8_one[:, :]).then_inc(ahead1_ready, 1)

                def a_edge(t):
                    act.wait_ge(masked_ready, HEADS * (t + 1))
                    nc.scalar.activation(edge[:, t, :], barred[:, t, :], ACT.Relu, bias=one[:, :],
                                         accum_out=outdeg[:, t:t + 1]).then_inc(edge_ready, 1)

                def b_affine(n, j):
                    affine(1, n, j, h, x, ACT.Relu, h_ready)
                    high_part(high, h, j, h_ready, TILES * n + PER_HALF * (j + 1), high_ready)

                def a_gather(layer, k):
                    for j in range(HALVES) if k else ():
                        nc.scalar.activation(auT[:, 0, halves(j)[0]], wait_filled(act, f"u{layer}_{j}"),
                                             ACT.Copy).then_inc(sum_high, 1)

                def state_part(layer, j):
                    if layer == 0:
                        wait_drained(act, f"ahT1_{j}")
                    else:
                        act.wait_ge(dve_gate, ((layer - 1) * HALVES + j + 1) * 4)
                    nc.scalar.activation(ahT2[:, 0, halves(j)[0]], ahT[:, halves(j)[0]],
                                         ACT.Copy).then_inc(state_high, 1)

                def a_gates(layer, j):
                    g = 4 * j
                    for name, place, func, b_ in (("r", R, ACT.Tanh, 0), ("hn", X, ACT.Identity, 2),
                                                  ("z", Z, ACT.Tanh, 1)):
                        bank = wait_filled(act, f"{name}{layer}_{j}")
                        is_drained(nc.scalar.activation(gates[:, g + place, :], bank, func,
                                                        scale=0.5 / WSCALE, bias=half_b[:, b_:b_ + 1]), f"{name}{layer}_{j}")
                    wait_drained(act, f"in{layer}_{j}")
                    nc.scalar.activation(gates[:, g + N, :], gates[:, g + X, :], ACT.Tanh,
                                         bias=cols[:, BIH + 2:BIH + 3]).then_inc(act_gate, 1)

                def high_of(dst, j, name, done):
                    nc.scalar.activation(dst[:, halves(j)[1], :], in_tiles(wait_filled(act, name)),
                                         ACT.Copy).then_inc(done, 1)

                def a_edgeT(t):
                    if graph is not None:
                        act.wait_ge(pool_done, 1)
                    bank = wait_filled(act, f"edgeT_{t}")
                    is_drained(nc.scalar.activation(edgeT[:, t, :], bank.bitcast(f16), ACT.Copy), f"edgeT_{t}")

                def b_rank(t):
                    for j in range(HALVES):
                        name = f"rank_{t}_{j}"
                        is_drained(nc.scalar.activation(edgeT[:, t, halves(j)[0]], wait_filled(act, name), ACT.Copy),
                                   name)

                def b_degrec():
                    to_T("degrec", degrec)

                def b_conv(c, j):
                    act.wait_ge(elu_dve, (c * HALVES + j) * 2 + 1)
                    nc.scalar.activation(elu[:, 2 * j, :], elu[:, 2 * j, :], ACT.Exp).then_inc(elu_act, 1)

                for stage in ORDER:
                    name, args = stage[0], stage[1:]
                    if name == "a_turnh":
                        to_T(f"ahT{args[0]}", ahT)
                        for j in range(HALVES) if args[0] else ():
                            state_part(0, j)
                    elif name in ("a_q", "a_k"):
                        a_part("qk".index(name[2]))
                    elif name == "a_step":
                        a_step(*args)
                    elif name == "a_ahead1":
                        a_ahead1(*args)
                    elif name == "a_ynorm":
                        for j in range(HALVES):
                            affine(0, 0, j, ah, ah, ACT.Identity, ynorm_ready)
                    elif name == "a_affine":
                        a_affine(*args)
                    elif name == "c_affine":
                        affine(2, 0, *args, ah, ah, ACT.Relu, next_ready)
                    elif name == "a_gather":
                        a_gather(*args)
                    elif name == "a_gates":
                        a_gates(*args)
                    elif name == "a_edge":
                        a_edge(*args)
                    elif name == "a_natural" and args[0] < LAYERS - 1:
                        high_of(ahigh, args[1], f"nat{args[0]}_{args[1]}", ahigh_ready)
                        state_part(args[0] + 1, args[1])
                    elif name == "a_edgeT":
                        a_edgeT(*args)
                    elif name == "b_affine":
                        b_affine(*args)
                    elif name == "b_rank":
                        b_rank(*args)
                    elif name == "b_turnh":
                        to_T(f"hT{args[0]}", hT)
                    elif name == "b_degrec":
                        b_degrec()
                    elif name == "b_conv":
                        b_conv(*args)
                    elif name == "b_cnatural" and args[0] < CONVS - 1:
                        high_of(high, args[1], f"cnat{args[0]}_{args[1]}", high_ready)

            @block.tensor
            def _(pe):
                def fill(name):
                    bank, before, _, empty = place_of(name)
                    if before:
                        pe.wait_ge(empty, before)
                    return bank

                def is_full(ins, name):
                    ins.then_inc(place_of(name)[2], 1)

                def turn_half(name, j, src):
                    bank = fill(name)
                    for t in range(PER_HALF):
                        last = nc.tensor.transpose(bank[:, t * P:(t + 1) * P], src(j * PER_HALF + t), ident[:, :])
                    is_full(last, name)

                def in_T(src):
                    return lambda t: src[:, t * P:(t + 1) * P]

                def gather(name, k, parts, mask):
                    for j in range(HALVES):
                        bank = place_of(f"{name}_{j}")[0] if k else fill(f"{name}_{j}")
                        for t in range(k * PER_HALF, (k + 1) * PER_HALF):
                            for i, part in enumerate(parts):
                                last = nc.tensor.matmul(bank, part[:, t, :], mask[:, t, halves(j)[0]],
                                                        start=(t == 0 and i == 0), stop=(t == TILES - 1 and i == 1))
                        if k:
                            is_full(last, f"{name}_{j}")

                def a_turnh(n):
                    for j in range(HALVES):
                        if n:
                            pe.wait_ge(ah_ready, PER_HALF * (j + 1))
                        turn_half(f"ahT{n}_{j}", j, lambda t: ah[:, t, :])

                def a_part(name, w):
                    for j in range(HALVES):
                        wait_drained(pe, f"ahT0_{j}")
                        bank = fill(f"{name}_{j}")
                        is_full(nc.tensor.matmul(bank, w[:, :], ahT[:, halves(j)[0]], start=True, stop=True),
                                f"{name}_{j}")

                def a_v():
                    for j in range(HALVES):
                        bank = fill(f"v_{j}")
                        for t in range(PER_HALF):
                            last = nc.tensor.matmul(bank[:, t * P:(t + 1) * P], in_T(ahT)(j * PER_HALF + t), wv[:, :],
                                                    start=True, stop=True)
                        is_full(last, f"v_{j}")

                def scores(s):
                    t, hd = s // HEADS, s % HEADS
                    if s < HEADS:
                        pe.wait_ge(stacked[hd], 16 * 4)
                    if s == 0:
                        for bank in (0, 1):
                            pe.wait_ge(drained["a"][bank], used_before(("a_step", 0), "a", bank))
                    else:
                        pe.wait_ge(masked_ready, s)
                    for j in range(HALVES):
                        last = nc.tensor.matmul(S[:, halves(j)[0]], qs[:, hd, t * P:(t + 1) * P],
                                                ks[:, hd, halves(j)[0]], start=True, stop=True)
                    last.then_inc(scores_ready, 1)

                def turn_probs(s):
                    pe.wait_ge(probs_ready, s + 1)
                    for j in range(2):
                        if s:
                            pe.wait_ge(probT_ready[j], s)
                        else:
                            pe.wait_ge(drained["a"][2 + j], used_before(("a_step", 0), "a", 2 + j))
                        for t in range(PER_HALF):
                            m = j * PER_HALF + t
                            last = nc.tensor.transpose(PT[:, j, t * P:(t + 1) * P],
                                                       prob[:, s % 2, m * P:(m + 1) * P], ident[:, :])
                        last.then_inc(turned[j], 1)

                def weigh(t, k):
                    if t == 0:
                        wait_drained(pe, "v_0", "v_1")
                    elif k == 0:
                        pe.wait_ge(sum_kept, t)
                    if k == 0:
                        for j in range(2):
                            pe.wait_ge(probT_ready[j], HEADS * (t + 1))
                    for m in range(k * PER_HALF, (k + 1) * PER_HALF):
                        for hd in range(HEADS):
                            last = nc.tensor.matmul(O[HEAD * hd:HEAD * (hd + 1), 0:P],
                                                    v[:, m, HEAD * hd:HEAD * (hd + 1)],
                                                    probT[:, (t * HEADS + hd) % RING, m, :],
                                                    start=(m == 0), stop=(m == TILES - 1))
                    if k:
                        last.then_inc(summed, 1)

                def a_step(s):
                    if s < STEPS:
                        scores(s)

                def a_turn(s):
                    if s > HEADS and s % HEADS == 2:
                        weigh(s // HEADS - 1, 1)
                    if 1 <= s <= STEPS:
                        turn_probs(s - 1)
                    if s > HEADS and s % HEADS == 1:
                        weigh(s // HEADS - 1, 0)

                def a_rinv():
                    pe.wait_ge(masked_ready, STEPS)
                    for j in range(2):
                        pe.wait_ge(probT_ready[j], STEPS)
                    pe.wait_ge(rwide_ready, 1)
                    for j in range(HALVES):
                        turn_half(f"rinvT_{j}", j, lambda t: rwide[:, t, :, :].rearrange("p a b -> p (a b)"))

                def a_y():
                    for j in range(HALVES):
                        pe.wait_ge(att_ready, j + 1)
                        bank = fill(f"y_{j}")
                        for t in range(PER_HALF):
                            last = nc.tensor.matmul(bank[:, t * P:(t + 1) * P], in_T(attU)(j * PER_HALF + t), wo[:, :],
                                                    start=True, stop=True)
                        is_full(last, f"y_{j}")

                def b_turnh(n):
                    for j in range(HALVES):
                        pe.wait_ge(h_ready, TILES * n + PER_HALF * (j + 1))
                        turn_half(f"hT{n}_{j}", j, lambda t: h[:, t, :])

                def a_gather(layer, k):
                    if layer == 0:
                        pe.wait_ge(alow_ready, k + 1)
                        pe.wait_ge(edge_ready, TILES)
                    else:
                        wait_drained(pe, f"nat{layer - 1}_{k}")
                    gather(f"u{layer}", k, (ahigh, alow), edge)

                def a_gates(layer, j):
                    half = halves(j)[0]
                    wait_drained(pe, f"u{layer}_{j}")
                    pe.wait_ge(state_low, layer * HALVES + j + 1)

                    def gate(name, g, *sides):
                        bank = fill(f"{name}{layer}_{j}")
                        passes = [(w[:, a, g * DIM:(g + 1) * DIM], src[:, b, half])
                                  for w, src in sides for a, b in ((0, 0), (0, 1), (1, 0))]
                        for k, (w, src) in enumerate(passes):
                            last = nc.tensor.matmul(bank, w, src, start=(k == 0), stop=(k == len(passes) - 1))
                        is_full(last, f"{name}{layer}_{j}")

                    wu = wgate[:, :, layer, :]
                    gate("r", 0, (wu, auT), (whh2, ahT2))
                    gate("hn", 2, (whh2, ahT2))
                    gate("in", 2, (wu, auT))
                    gate("z", 1, (wu, auT), (whh2, ahT2))

                def a_natural(layer, j):
                    pe.wait_ge(dve_gate, (layer * HALVES + j + 1) * 4)
                    turn_half(f"nat{layer}_{j}", j, in_T(ahT))

                def a_edgeT(t):
                    pe.wait_ge(limited, 1)
                    bank = fill(f"edgeT_{t}").bitcast(f16)
                    for n in range(TILES):
                        last = nc.tensor.transpose(bank[:, n * P:(n + 1) * P], edge[:, n, t * P:(t + 1) * P],
                                                   ident16[:, :])
                    is_full(last, f"edgeT_{t}")

                def b_counts():
                    bank = fill("counts")
                    for t in range(TILES):
                        for n in range(TILES):
                            last = nc.tensor.matmul(bank[:, t * TILES + n:t * TILES + n + 1],
                                                    edgeT[:, t, n * P:(n + 1) * P], ones16[:, 0:1],
                                                    start=True, stop=True)
                    is_full(last, "counts")

                def b_rank(t):
                    for j in range(HALVES):
                        bank = fill(f"rank_{t}_{j}")
                        is_full(nc.tensor.matmul(bank, before[:, :], edgeT[:, t, halves(j)[0]],
                                                 start=True, stop=True), f"rank_{t}_{j}")

                def pick(bank, t, half, hot):
                    nc.tensor.matmul(bank, high[:, t, :], hot[:, half], start=True, stop=False)
                    return nc.tensor.matmul(bank, low[:, t, :], hot[:, half], start=False, stop=True)

                def b_slot(i):
                    if i == 0:
                        pe.wait_ge(low_ready, HALVES)
                    pe.wait_ge(onehot_ready, i + 1)
                    for j in range(HALVES):
                        name = f"slot{i}_{j}"
                        is_full(pick(fill(name), i // FIXED, halves(j)[0], onehot[:, i % 2, :]), name)

                def b_extra():
                    for bank in range(HALVES):
                        pe.wait_ge(drained["b"][bank], used_before(("b_extra",), "b", bank))
                    pe.wait_ge(table_ready, 3)
                    more = pe.value_load(more_i[0:1, 0:1], min_val=0, max_val=(SLOTS - FIXED) * TILES)
                    with pe.If(more > 0):
                        for t in range(TILES):
                            extra = pe.value_load(extra_i[0:1, t:t + 1], min_val=0, max_val=SLOTS - FIXED)
                            first = pe.value_load(first_i[0:1, t:t + 1], min_val=0, max_val=(SLOTS - FIXED) * TILES)
                            with pe.If(extra > 0):
                                with pe.Fori(0, extra) as k:
                                    pe.wait_ge(extra_ready, first + (k + 1))
                                    for j in range(HALVES):
                                        pick(G[:, j, :], t, halves(j)[0], onehot[:, 0, :]).then_inc(picked[j], 1)
                    pe.wait_ge(pool_done, 1)

                def b_pool():
                    wait_drained(pe, "hT0_0", "hT0_1")
                    for j in range(HALVES):
                        bank = fill(f"pool_{j}")
                        for t in range(PER_HALF):
                            o, n = bank[:, t * P:(t + 1) * P], j * PER_HALF + t
                            nc.tensor.matmul(o, in_T(hT)(n), wpool[:, 0, :], start=True, stop=False)
                            last = nc.tensor.matmul(o, in_T(uT)(n), wpool[:, 1, :], start=False, stop=True)
                        is_full(last, f"pool_{j}")

                def b_degree():
                    pe.wait_ge(edge1_ready, 16)
                    bank = fill("degcol")
                    for t in range(TILES):
                        for n in range(TILES):
                            last = nc.tensor.matmul(bank[:, t:t + 1], edge1[:, n, t * P:(t + 1) * P].bitcast(f8),
                                                    ones16[:, 0:1], start=(n == 0), stop=(n == TILES - 1))
                    is_full(last, "degcol")

                def b_degrec():
                    pe.wait_ge(degwide_ready, 1)
                    for j in range(HALVES):
                        turn_half(f"degrec_{j}", j, lambda t: degwide[:, t, :])

                def b_cgather(c, k):
                    if c == 0:
                        pe.wait_ge(low_ready, HALVES + k + 1)
                    else:
                        wait_drained(pe, f"cnat{c - 1}_{k}")
                    gather(f"cu{c}", k, (high, low), edge1[:, :, :].bitcast(f8))

                def b_conv(c, j):
                    if c == 0:
                        wait_drained(pe, f"hT1_{j}")
                    wait_drained(pe, f"cu{c}_{j}")
                    bank, half = fill(f"cy{c}_{j}"), halves(j)[0]
                    nc.tensor.matmul(bank, wroot[:, c, :], hT[:, half], start=True, stop=False)
                    is_full(nc.tensor.matmul(bank, wrel[:, c, :], uT[:, half], start=False, stop=True), f"cy{c}_{j}")

                def b_cnatural(c, j):
                    pe.wait_ge(elu_dve, (c * HALVES + j) * 2 + 2)
                    turn_half(f"cnat{c}_{j}", j, in_T(hT))

                for stage in ORDER:
                    name, args = stage[0], stage[1:]
                    if name == "a_turnh":
                        a_turnh(*args)
                    elif name == "a_q":
                        a_part("q", wq)
                    elif name == "a_k":
                        a_part("k", wk)
                    elif name == "a_v":
                        a_v()
                    elif name == "a_step":
                        a_step(*args)
                    elif name == "a_turn":
                        a_turn(*args)
                    elif name == "a_rinv":
                        a_rinv()
                    elif name == "a_y":
                        a_y()
                    elif name == "a_gather":
                        a_gather(*args)
                    elif name == "a_gates":
                        a_gates(*args)
                    elif name == "a_natural":
                        a_natural(*args)
                    elif name == "a_edgeT":
                        a_edgeT(*args)
                    elif name == "b_turnh":
                        b_turnh(*args)
                    elif name == "b_counts":
                        b_counts()
                    elif name == "b_rank":
                        b_rank(*args)
                    elif name == "b_slot":
                        b_slot(*args)
                    elif name == "b_extra":
                        b_extra()
                    elif name == "b_pool":
                        b_pool()
                    elif name == "b_degree":
                        b_degree()
                    elif name == "b_degrec":
                        b_degrec()
                    elif name == "b_cgather":
                        b_cgather(*args)
                    elif name == "b_conv":
                        b_conv(*args)
                    elif name == "b_cnatural":
                        b_cnatural(*args)

            @block.vector
            def _(dve):
                small = [0]

                def link(ins):
                    small[0] += 1
                    ins.then_inc(dve_small, 1)
                    dve.wait_ge(dve_small, small[0])

                def mean_and_var(w, n, src):
                    for t in range(TILES):
                        nc.vector.bn_stats(stats[w][:, t, :], src[:, t, :]).then_inc(stats_ready[w], 1)
                    for t in range(TILES):
                        dve.wait_ge(stats_ready[w], TILES * n + t + 1)
                        nc.vector.bn_aggr(meanvar[w][:, t, :], stats[w][:, t, :]).then_inc(meanvar_ready[w], 1)

                def shift_of(w, n):
                    dve.wait_ge(rstd_ready[w], n + 1)
                    nc.vector.scalar_tensor_tensor(shift[w][:, :], meanvar[w][:, :, 0], -1.0, rstd[w][:, :],
                                                   op0=ALU.mult, op1=ALU.mult).then_inc(shift_ready[w], 1)

                def add_row(name, dst, row):
                    for j in range(HALVES):
                        bank = wait_filled(dve, f"{name}_{j}")
                        is_drained(nc.vector.tensor_tensor(
                            dst[:, halves(j)[1], :], in_tiles(bank),
                            rows[:, row:row + 1, :].to_broadcast([P, PER_HALF, DIM]), op=ALU.add), f"{name}_{j}")

                def a_stats(n):
                    if n == 0:
                        wait_drained(dve, "y_0", "y_1")
                    mean_and_var(0, n, (ah, ax)[n])

                def a_part(i):
                    for j in range(HALVES):
                        half = halves(j)[0]
                        dve.wait_ge(part_high, HALVES * i + j + 1)
                        nc.vector.tensor_tensor(parts[i][1][:, half], qk32[i][:, half], parts[i][0][:, half],
                                                op=ALU.subtract).then_inc(part_low, 1)

                def a_step(s):
                    if s < STEPS:
                        dve.wait_ge(scores_ready, s + 1)
                        dve.wait_ge(barred_ready, s // HEADS + 1)
                        if s >= 2:
                            dve.wait_ge(probs_ready, s - 1)
                        nc.vector.tensor_tensor_reduce(out=masked[:, s % 2, :], in0=S[:, :],
                                                       in1=barred[:, s // HEADS, :], scale=-1.0, scalar=3.0e38,
                                                       op0=ALU.add, op1=ALU.min,
                                                       accum_out=negmax[:, s:s + 1]).then_inc(masked_ready, 1)
                    if s > HEADS and s % HEADS == 3:
                        keep_sum(s // HEADS - 1)

                def keep_sum(t):
                    dve.wait_ge(summed, t + 1)
                    nc.vector.tensor_copy(attU[:, t * P:(t + 1) * P], O[:, 0:P]).then_inc(sum_kept, 1)

                def a_rinv():
                    keep_sum(TILES - 1)
                    dve.wait_ge(probs_ready, STEPS)
                    link(nc.vector.reciprocal(rinv[:, :], rowsum[:, :]))
                    nc.vector.tensor_copy(rwide[:, :, :, :].rearrange("p a b c -> p (a b) c"),
                                          rinv[:, :].unsqueeze(2).to_broadcast([P, STEPS, HEAD]))\
                        .then_inc(rwide_ready, 1)
                    dve.wait_ge(sum_kept, TILES)
                    for j in range(HALVES):
                        half, name = halves(j)[0], f"rinvT_{j}"
                        nc.vector.tensor_tensor(attU[:, half], attU[:, half], wait_filled(dve, name),
                                                op=ALU.mult).then_inc(att_ready, 1)
                        dve.wait_ge(att_ready, j + 1)
                        dve.sem_inc(place_of(name)[3], 1)

                def a_gain():
                    dve.wait_ge(ynorm_ready, TILES)
                    link(nc.vector.tensor_tensor(ah[:, :, :], ah[:, :, :],
                                                 rows[:, GAMMA:GAMMA + 1, :].to_broadcast([P, TILES, DIM]),
                                                 op=ALU.mult))
                    dve.wait_ge(beta_added, 1)
                    link(nc.vector.tensor_tensor(ax[:, :, :], ax[:, :, :], ah[:, :, :], op=ALU.add))

                def a_end():
                    wait_drained(dve, *(f"nat{LAYERS - 1}_{j}" for j in range(HALVES)))
                    if graph is not None:
                        wait_drained(dve, *(f"cnat{CONVS - 1}_{j}" for j in range(HALVES)))
                    nc.vector.tensor_copy(x[:, :, :], ax[:, :, :]).then_inc(ax_ready, 1)

                def a_gather(layer, k):
                    for j in range(HALVES) if k else ():
                        name = f"u{layer}_{j}"
                        bank = wait_filled(dve, name)
                        dve.wait_ge(sum_high, layer * HALVES + j + 1)
                        is_drained(nc.vector.tensor_tensor(auT[:, 1, halves(j)[0]], bank, auT[:, 0, halves(j)[0]],
                                                           op=ALU.subtract), name)

                def state_part(layer, j):
                    half = halves(j)[0]
                    dve.wait_ge(state_high, layer * HALVES + j + 1)
                    nc.vector.tensor_tensor(ahT2[:, 1, half], ahT[:, half], ahT2[:, 0, half],
                                            op=ALU.subtract).then_inc(state_low, 1)

                def low_part(dst, src, highs, j, high_is, count, done):
                    dve.wait_ge(high_is, count)
                    nc.vector.tensor_tensor(dst[:, halves(j)[1], :], src[:, halves(j)[1], :], highs[:, halves(j)[1], :],
                                            op=ALU.subtract).then_inc(done, 1)

                def a_affine(j):
                    if j == 0:
                        shift_of(0, 1)
                    low_part(alow, ah, ahigh, j, ahigh_ready, j + 1, alow_ready)

                def b_affine(n, j):
                    if j == 0:
                        shift_of(1, n)
                    low_part(low, h, high, j, high_ready, HALVES * n + j + 1, low_ready)

                def a_gates(layer, j):
                    g, half, step = 4 * j, halves(j)[0], (layer * HALVES + j) * 4
                    wait_drained(dve, f"r{layer}_{j}", f"hn{layer}_{j}")
                    nc.vector.scalar_tensor_tensor(gates[:, g + X, :], gates[:, g + R, :], 1.0, gates[:, g + X, :],
                                                   op0=ALU.add, op1=ALU.mult).then_inc(dve_gate, 1)
                    dve.wait_ge(dve_gate, step + 1)
                    is_drained(nc.vector.scalar_tensor_tensor(
                        gates[:, g + X, :], wait_filled(dve, f"in{layer}_{j}"), 1.0 / WSCALE, gates[:, g + X, :],
                        op0=ALU.mult, op1=ALU.add), f"in{layer}_{j}")
                    dve.wait_ge(act_gate, layer * HALVES + j + 1)
                    nc.vector.tensor_tensor(gates[:, g + R, :], ahT[:, half], gates[:, g + N, :],
                                            op=ALU.subtract).then_inc(dve_gate, 1)
                    dve.wait_ge(dve_gate, step + 2)
                    nc.vector.scalar_tensor_tensor(gates[:, g + R, :], gates[:, g + Z, :], 1.0, gates[:, g + R, :],
                                                   op0=ALU.add, op1=ALU.mult).then_inc(dve_gate, 1)
                    dve.wait_ge(dve_gate, step + 3)
                    nc.vector.scalar_tensor_tensor(ahT[:, half], gates[:, g + R, :], 0.5, gates[:, g + N, :],
                                                   op0=ALU.mult, op1=ALU.add).then_inc(dve_gate, 1)

                def low_of(dst, highs, j, name, high_is, high_count):
                    bank, tiles = in_tiles(wait_filled(dve, name)), halves(j)[1]
                    dve.wait_ge(high_is, high_count + j)
                    is_drained(nc.vector.tensor_tensor(dst[:, tiles, :], bank, highs[:, tiles, :],
                                                       op=ALU.subtract), name)

                def add_to(dst, src, j, name):
                    bank, tiles = in_tiles(wait_filled(dve, name)), halves(j)[1]
                    is_drained(nc.vector.tensor_tensor(dst[:, tiles, :], src[:, tiles, :], bank, op=ALU.add), name)

                def a_barred(t):
                    dve.wait_ge(raw_loaded[t % 2], 16 * (t // 2 + 1))
                    nc.vector.tensor_scalar(barred[:, t, :], raw[:, t % 2, :], 0.0, -BIG, op0=ALU.is_equal,
                                            op1=ALU.mult).then_inc(barred_ready, 1)

                def a_maxdeg():
                    dve.wait_ge(edge_ready, TILES)
                    nc.vector.tensor_reduce(maxdeg[:, :], outdeg[:, :], axis=AX.X, op=ALU.max).then_inc(edge_ready, 1)

                def a_limit():
                    last = f"u{LAYERS - 1}"
                    wait_filled(dve, f"{last}_0")
                    wait_filled(dve, f"{last}_1")
                    dve.wait_ge(maxdeg_ready, 1)
                    link(nc.vector.tensor_copy(maxdeg_i[:, :], maxdeg_all[0:1, :]))
                    most = dve.value_load(maxdeg_i[0:1, 0:1], min_val=0, max_val=NODES)
                    with dve.If(most > SLOTS):
                        for t in range(TILES):
                            nc.vector.tensor_tensor_scan(count[:, :], ones_row[:, :], edge[:, t, :], 0.0, ALU.mult,
                                                         ALU.add).then_inc(limit_step, 1)
                            dve.wait_ge(limit_step, 2 * t + 1)
                            nc.vector.scalar_tensor_tensor(edge[:, t, :], count[:, :], float(SLOTS), edge[:, t, :],
                                                           op0=ALU.is_le, op1=ALU.mult).then_inc(limit_step, 1)
                            dve.wait_ge(limit_step, 2 * t + 2)
                    dve.sem_inc(limited, 1)

                def b_counts():
                    is_drained(nc.vector.tensor_reduce(
                        slots_f[:, :], wait_filled(dve, "counts")[:, 0:TILES * TILES]
                        .rearrange("p (t n) -> p t n", t=TILES), axis=AX.X, op=ALU.max), "counts")

                def b_table():
                    dve.wait_ge(slots_known, 1)
                    link(nc.vector.tensor_scalar(slots_all[0:1, :], slots_all[0:1, :], -float(FIXED), 0.0,
                                                 op0=ALU.add, op1=ALU.max))
                    link(nc.vector.tensor_tensor_scan(first_f[:, :], ones_row[0:1, 0:TILES], slots_all[0:1, :], 0.0,
                                                      ALU.mult, ALU.add))
                    nc.vector.tensor_copy(extra_i[:, :], slots_all[0:1, :]).then_inc(table_ready, 1)
                    nc.vector.tensor_copy(more_i[:, :], first_f[:, TILES - 1:TILES]).then_inc(table_ready, 1)
                    nc.vector.tensor_tensor(first_i[:, :], first_f[:, :], slots_all[0:1, :],
                                            op=ALU.subtract).then_inc(table_ready, 1)

                def b_first():
                    link(nc.vector.memset(uT[:, :], 0.0))
                    set_onehot(0)

                def set_onehot(i):
                    if i % FIXED == 0:
                        wait_drained(dve, *(f"rank_{i // FIXED}_{j}" for j in range(HALVES)))
                    nc.vector.tensor_scalar(onehot[:, i % 2, :], edgeT[:, i // FIXED, :],
                                            slotnum[:, i % FIXED:i % FIXED + 1], None,
                                            op0=ALU.is_equal).then_inc(onehot_ready, 1)

                def b_slot(i):
                    if i + 1 < TILES * FIXED:
                        if i:
                            wait_filled(dve, f"slot{i - 1}_{HALVES - 1}")
                        set_onehot(i + 1)
                    for j in range(HALVES):
                        half, name = halves(j)[0], f"slot{i}_{j}"
                        if i:
                            wait_drained(dve, f"slot{i - 1}_{j}")
                        is_drained(nc.vector.tensor_tensor(uT[:, half], uT[:, half], wait_filled(dve, name),
                                                           op=ALU.max), name)

                def b_extra():
                    wait_drained(dve, *(f"slot{TILES * FIXED - 1}_{j}" for j in range(HALVES)))
                    dve.wait_ge(table_ready, 3)
                    for j in range(HALVES):
                        dve.sem_inc(pooled[j], 1)
                    more = dve.value_load(more_i[0:1, 0:1], min_val=0, max_val=(SLOTS - FIXED) * TILES)
                    with dve.If(more > 0):
                        for t in range(TILES):
                            extra = dve.value_load(extra_i[0:1, t:t + 1], min_val=0, max_val=SLOTS - FIXED)
                            first = dve.value_load(first_i[0:1, t:t + 1], min_val=0, max_val=(SLOTS - FIXED) * TILES)
                            with dve.If(extra > 0):
                                with dve.Fori(0, extra) as k:
                                    for j in range(HALVES):
                                        dve.wait_ge(pooled[j], first + (k + 1))
                                    nc.vector.tensor_scalar(onehot[:, 0, :], edgeT[:, t, :],
                                                            slotnum[:, bass.ds(k + FIXED, 1)], None,
                                                            op0=ALU.is_equal).then_inc(extra_ready, 1)
                                    for j in range(HALVES):
                                        half = halves(j)[0]
                                        dve.wait_ge(picked[j], first + (k + 1))
                                        nc.vector.tensor_tensor(uT[:, half], uT[:, half], G[:, j, :],
                                                                op=ALU.max).then_inc(pooled[j], 1)
                        for j in range(HALVES):
                            dve.wait_ge(pooled[j], more + 1)
                        dve.sem_inc(extra_ready, 1)
                    dve.sem_inc(pool_done, 1)

                def b_pool():
                    add_row("pool", h, BPOOL)
                    wait_drained(dve, "pool_0", "pool_1")
                    link(nc.vector.scalar_tensor_tensor(x[:, :, :], h[:, :, :], 0.0, x[:, :, :],
                                                        op0=ALU.max, op1=ALU.add))

                def b_degree():
                    is_drained(nc.vector.tensor_scalar(deg[:, :], wait_filled(dve, "degcol")[:, 0:TILES], 1.0, None,
                                                       op0=ALU.max), "degcol")
                    wait_drained(dve, "degcol")
                    link(nc.vector.reciprocal(deg[:, :], deg[:, :]))
                    nc.vector.tensor_copy(degwide[:, :, :],
                                          deg[:, :].unsqueeze(2).to_broadcast([P, TILES, P])).then_inc(degwide_ready, 1)

                def b_cgather(c, k):
                    for j in range(HALVES) if k else ():
                        bank, half = wait_filled(dve, f"cu{c}_{j}"), halves(j)[0]
                        wait_drained(dve, f"degrec_{j}")
                        is_drained(nc.vector.tensor_tensor(uT[:, half], bank, degrec[:, half], op=ALU.mult),
                                   f"cu{c}_{j}")

                def b_conv(c, j):
                    bias, half, name = cols[:, BCONV + c:BCONV + c + 1], halves(j)[0], f"cy{c}_{j}"
                    bank = wait_filled(dve, name)
                    nc.vector.tensor_scalar(elu[:, 2 * j, :], bank, bias, 0.0, op0=ALU.add,
                                            op1=ALU.min).then_inc(elu_dve, 1)
                    is_drained(nc.vector.tensor_scalar(elu[:, 2 * j + 1, :], bank, bias, 0.0, op0=ALU.add,
                                                       op1=ALU.max), name)
                    wait_drained(dve, name)
                    dve.wait_ge(elu_act, c * HALVES + j + 1)
                    nc.vector.scalar_tensor_tensor(hT[:, half], elu[:, 2 * j, :], -1.0, elu[:, 2 * j + 1, :],
                                                   op0=ALU.add, op1=ALU.add).then_inc(elu_dve, 1)

                for stage in ORDER:
                    name, args = stage[0], stage[1:]
                    if name == "a_stats":
                        a_stats(*args)
                    elif name == "a_affine":
                        a_affine(*args)
                    elif name == "c_stats":
                        dve.wait_ge(next_loaded, 16)
                        mean_and_var(2, 0, ah)
                    elif name == "c_affine" and args[0] == 0:
                        shift_of(2, 0)
                    elif name in ("a_q", "a_k"):
                        a_part("qk".index(name[2]))
                    elif name == "a_v":
                        add_row("v", v, BV)
                    elif name == "a_step":
                        a_step(*args)
                    elif name == "a_rinv":
                        a_rinv()
                    elif name == "a_y":
                        add_row("y", ah, BO)
                    elif name == "a_ynorm":
                        shift_of(0, 0)
                    elif name == "a_gain":
                        a_gain()
                    elif name == "a_turnh" and args[0]:
                        for j in range(HALVES):
                            state_part(0, j)
                    elif name == "a_gather":
                        a_gather(*args)
                    elif name == "a_gates":
                        a_gates(*args)
                    elif name == "a_natural":
                        if args[0] < LAYERS - 1:
                            low_of(alow, ahigh, args[1], f"nat{args[0]}_{args[1]}", ahigh_ready, 3 + HALVES * args[0])
                            state_part(args[0] + 1, args[1])
                        else:
                            add_to(ax, ax, args[1], f"nat{args[0]}_{args[1]}")
                    elif name == "a_barred":
                        a_barred(*args)
                    elif name == "a_maxdeg":
                        a_maxdeg()
                    elif name == "a_limit":
                        a_limit()
                    elif name == "b_stats":
                        mean_and_var(1, args[0], x)
                    elif name == "b_affine":
                        b_affine(*args)
                    elif name == "b_counts":
                        b_counts()
                    elif name == "b_table":
                        b_table()
                    elif name == "b_first":
                        b_first()
                    elif name == "b_slot":
                        b_slot(*args)
                    elif name == "b_extra":
                        b_extra()
                    elif name == "b_pool":
                        b_pool()
                    elif name == "b_degree":
                        b_degree()
                    elif name == "b_cgather":
                        b_cgather(*args)
                    elif name == "b_conv":
                        b_conv(*args)
                    elif name == "b_cnatural":
                        if args[0] < CONVS - 1:
                            low_of(low, high, args[1], f"cnat{args[0]}_{args[1]}", high_ready, 5 + HALVES * args[0])
                        else:
                            add_to(h, x, args[1], f"cnat{args[0]}_{args[1]}")
                if ahead is not None:
                    a_end()

        def turn(following, ahead, graph):
            with nc.Block() as block:
                stages(block, following, ahead, graph)
            nc.all_engine_barrier(sems_to_clear=range(sems[0].num, sems[-1].num + 1))

        turn(0, None, None)
        turn(1, 0, None)
        with nc.Fori(0, BATCH - 2) as b:
            turn(b + 2, b + 1, b)
        turn(None, BATCH - 1, BATCH - 2)
        turn(None, None, BATCH - 1)


def kernel(**inputs):
    import numpy as np
    import concourse.bacc as bacc
    from concourse.bass_utils import run_bass_kernel_spmd

    a = {n: np.asarray(v) for n, v in inputs.items()}

    def column_blocks(v):
        return v.reshape(-1, 128).T

    layout = {
        "x": a["x"], "adj": a["adj"],
        "wqT": a["L0_gnn_Wq"].T, "wkT": a["L0_gnn_Wk"].T, "wvT": a["L0_gnn_Wv"].T, "woT": a["L0_gnn_Wo"].T,
        "wihT": a["L1_gnn_w_ih"].T, "whhT": a["L1_gnn_w_hh"].T,
        "wmsgT": a["L1_gnn_weight"].transpose(2, 0, 1),
        "wpool": a["L2_gnn_W"].reshape(2, 128, 128).transpose(1, 0, 2),
        "wroot": np.stack([a["L3_gnn_w_root1"], a["L3_gnn_w_root2"]], 1),
        "wrel": np.stack([a["L3_gnn_w_rel1"][1], a["L3_gnn_w_rel2"][1]], 1),
        "cols": np.concatenate([column_blocks(a[n]) for n in (
            "L0_gnn_bq", "L0_gnn_bk", "L1_gnn_b_ih", "L1_gnn_b_hh", "L3_gnn_b1", "L3_gnn_b2")], 1),
        "rows": np.broadcast_to(np.stack([a[n] for n in (
            "L0_gnn_bv", "L0_gnn_bo", "L0_gnn_gamma", "L0_gnn_beta", "L2_gnn_b")]), (128, 5, 128)),
    }
    nc = bacc.Bacc("TRN2", target_bir_lowering=False, num_devices=1)
    arrays, args = {}, {}
    for name, v in layout.items():
        v = np.ascontiguousarray(v)
        arrays[f"in_{name}_dram"] = v
        args[name] = nc.dram_tensor(f"in_{name}_dram", v.shape, mybir.dt.from_np(v.dtype), kind="ExternalInput").ap()
    out = nc.dram_tensor("out_0_dram", (BATCH, NODES, DIM), mybir.dt.float32, kind="ExternalOutput").ap()
    program(nc, args, out)
    r = run_bass_kernel_spmd(nc, [arrays], core_ids=[0])
    return r.results[0]["out_0_dram"]
```
